# Optimizing a Trainium2 kernel written in Bass

```python
import numpy as np
import jax
import jax.numpy as jnp

def _softmax(x, axis=-1):
    return jax.nn.softmax(x, axis=axis)

def _gelu(x):
    return jax.nn.gelu(x, approximate=True)

def _silu(x):
    return jax.nn.silu(x)

def _sigmoid(x):
    return jax.nn.sigmoid(x)

def _layernorm(x, axis=-1, eps=1e-05):
    m = jnp.mean(x, axis=axis, keepdims=True)
    v = jnp.var(x, axis=axis, keepdims=True)
    return (x - m) / jnp.sqrt(v + eps)

def _scatter_add(tgt, idx, src, axis=0):
    return tgt.at[idx].add(src)

def _segment_sum(src, seg, n):
    return jax.ops.segment_sum(src, seg, n)
kernel_name = 'mk_gnn_resnorm_d2_gnn_r8_234b8b'

def setup_inputs(seed: int=0):
    np.random.seed(seed)
    _w = jnp.asarray

    def _rec_inputs():
        import jax
        import jax.numpy as jnp
        _gk = jax.random.key(seed)
        x = -0.000202 + 1 * jax.random.normal(jax.random.fold_in(_gk, 1), (6250, 128), jnp.float32)
        _s = jax.random.randint(jax.random.fold_in(_gk, 2), (100000,), 0, 6250, jnp.int32)
        _d = jax.random.randint(jax.random.fold_in(_gk, 3), (100000,), 0, 6250, jnp.int32)
        _loop = jnp.arange(6250, dtype=jnp.int32)
        src = jnp.concatenate([_s, _d, _loop])
        dst = jnp.concatenate([_d, _s, _loop])
        _o = jnp.argsort(dst, stable=True)
        src = src[_o]
        dst = dst[_o]
        edge_attr_128 = -5.16925e-05 + 1.00005 * jax.random.normal(jax.random.fold_in(_gk, 11), (206250, 128), jnp.float32)
        return (x, src, dst, edge_attr_128)
    x, src, dst, edge_attr_128 = _rec_inputs()

    def _L0_gnn_setup():
        import jax, jax.numpy as jnp
        import numpy as np
        N = 6250
        E = 100000
        D = 128
        BN_EPS = 1e-05
        LN_EPS = 1e-05
        key = jax.random.key(seed)
        ks = jax.random.split(key, 8)
        s = 0.05
        return {'x': jax.random.normal(ks[0], (N, D), jnp.float32), 'edge_index': jax.random.randint(ks[1], (2, E), 0, N, dtype=jnp.int64), 'edge_attr': jax.random.normal(ks[2], (E, D), jnp.float32), 'eps': jnp.zeros((), jnp.float32), 'We': jax.random.normal(ks[3], (D, D), jnp.float32) * s, 'be': jnp.zeros((D,), jnp.float32), 'W1': jax.random.normal(ks[4], (D, D), jnp.float32) * s, 'b1': jnp.zeros((D,), jnp.float32), 'bn_g': jnp.ones((D,), jnp.float32), 'bn_b': jnp.zeros((D,), jnp.float32), 'bn_rm': jnp.zeros((D,), jnp.float32), 'bn_rv': jnp.ones((D,), jnp.float32), 'W2': jax.random.normal(ks[5], (D, D), jnp.float32) * s, 'b2': jnp.zeros((D,), jnp.float32), 'ln_g': jnp.ones((D,), jnp.float32), 'ln_b': jnp.zeros((D,), jnp.float32)}
    _L0_gnn_all = _L0_gnn_setup()
    _L0_gnn_in = {k: v for k, v in _L0_gnn_all.items() if k in ('eps', 'We', 'be', 'W1', 'b1', 'bn_g', 'bn_b', 'bn_rm', 'bn_rv', 'W2', 'b2', 'ln_g', 'ln_b')}
    del _L0_gnn_all

    def _L1_gnn_setup():
        import jax, jax.numpy as jnp
        import numpy as np
        N_NODES = 12500
        N_EDGES = 80000
        D_FEAT = 128
        key = jax.random.key(seed)
        k1, k2, k3, k4 = jax.random.split(key, 4)
        x = jax.random.normal(k1, (N_NODES, D_FEAT), dtype=jnp.float32)
        edge_index = jax.random.randint(k2, (2, N_EDGES), 0, N_NODES, dtype=jnp.int64)
        W = jax.random.normal(k3, (D_FEAT, D_FEAT), dtype=jnp.float32) / np.sqrt(D_FEAT)
        W_self = jax.random.normal(k4, (D_FEAT, D_FEAT), dtype=jnp.float32) / np.sqrt(D_FEAT)
        return {'x': x, 'edge_index': edge_index, 'W': W, 'W_self': W_self}
    _L1_gnn_all = _L1_gnn_setup()
    _L1_gnn_in = {k: v for k, v in _L1_gnn_all.items() if k in ('W', 'W_self')}
    del _L1_gnn_all
    return {'x': x, 'src': src, 'dst': dst, 'edge_attr_128': edge_attr_128, 'L0_gnn_eps': _L0_gnn_in['eps'], 'L0_gnn_We': _L0_gnn_in['We'], 'L0_gnn_be': _L0_gnn_in['be'], 'L0_gnn_W1': _L0_gnn_in['W1'], 'L0_gnn_b1': _L0_gnn_in['b1'], 'L0_gnn_bn_g': _L0_gnn_in['bn_g'], 'L0_gnn_bn_b': _L0_gnn_in['bn_b'], 'L0_gnn_bn_rm': _L0_gnn_in['bn_rm'], 'L0_gnn_bn_rv': _L0_gnn_in['bn_rv'], 'L0_gnn_W2': _L0_gnn_in['W2'], 'L0_gnn_b2': _L0_gnn_in['b2'], 'L0_gnn_ln_g': _L0_gnn_in['ln_g'], 'L0_gnn_ln_b': _L0_gnn_in['ln_b'], 'L1_gnn_W': _L1_gnn_in['W'], 'L1_gnn_W_self': _L1_gnn_in['W_self']}

def reference(x, src, dst, edge_attr_128, L0_gnn_eps, L0_gnn_We, L0_gnn_be, L0_gnn_W1, L0_gnn_b1, L0_gnn_bn_g, L0_gnn_bn_b, L0_gnn_bn_rm, L0_gnn_bn_rv, L0_gnn_W2, L0_gnn_b2, L0_gnn_ln_g, L0_gnn_ln_b, L1_gnn_W, L1_gnn_W_self):
    import jax
    import jax.numpy as jnp

    def _L0_gnn_ref(x, edge_index, edge_attr, eps, We, be, W1, b1, bn_g, bn_b, bn_rm, bn_rv, W2, b2, ln_g, ln_b):
        import jax, jax.numpy as jnp
        import numpy as np
        N = 6250
        E = 100000
        D = 128
        BN_EPS = 1e-05
        LN_EPS = 1e-05
        src, dst = (edge_index[0], edge_index[1])
        msg = jax.nn.relu(x[src] + edge_attr @ We.T + be)
        aggr = jax.ops.segment_sum(msg, dst, num_segments=N)
        h = (1.0 + eps) * x + aggr
        h = h @ W1.T + b1
        h = (h - bn_rm) * jax.lax.rsqrt(bn_rv + BN_EPS) * bn_g + bn_b
        h = jax.nn.relu(h)
        h = h @ W2.T + b2
        mu = jnp.mean(h, axis=-1, keepdims=True)
        var = jnp.mean(jnp.square(h - mu), axis=-1, keepdims=True)
        h = (h - mu) * jax.lax.rsqrt(var + LN_EPS) * ln_g + ln_b
        return jax.nn.relu(h + x)

    def _L1_gnn_ref(x, edge_index, W, W_self):
        import jax, jax.numpy as jnp
        import numpy as np
        N_NODES = 12500
        N_EDGES = 80000
        D_FEAT = 128
        src = edge_index[0]
        tgt = edge_index[1]
        messages = jnp.take(x, src, axis=0) @ W
        aggr_out = jax.ops.segment_sum(messages, tgt, num_segments=x.shape[0])
        return aggr_out + x @ W_self
    edge_index = jnp.stack([src, dst])
    x = _layernorm(x + _L0_gnn_ref(x, edge_index, edge_attr_128, L0_gnn_eps, L0_gnn_We, L0_gnn_be, L0_gnn_W1, L0_gnn_b1, L0_gnn_bn_g, L0_gnn_bn_b, L0_gnn_bn_rm, L0_gnn_bn_rv, L0_gnn_W2, L0_gnn_b2, L0_gnn_ln_g, L0_gnn_ln_b), axis=-1)
    x = _layernorm(x + _L1_gnn_ref(x, edge_index, L1_gnn_W, L1_gnn_W_self), axis=-1)
    return x

_drawn_inputs = setup_inputs


def setup_inputs(seed=0):
    import zlib

    import numpy as np

    out = dict(_drawn_inputs(seed))
    spreads = {'L0_gnn_be': (0.0, 0.1),
     'L0_gnn_b1': (0.0, 0.701),
     'L0_gnn_bn_g': (1.0, 0.2),
     'L0_gnn_bn_b': (0.0, 0.643),
     'L0_gnn_bn_rm': (0.0, 0.626),
     'L0_gnn_bn_rv': (1.0, 0.2),
     'L0_gnn_b2': (0.0, 0.331),
     'L0_gnn_ln_g': (1.0, 0.2),
     'L0_gnn_ln_b': (0.0, 0.1)}
    factors = {}
    for name, (base, spread) in spreads.items():
        noise = np.random.default_rng([zlib.crc32(name.encode()), seed]).standard_normal(out[name].shape)
        drawn = base * np.exp(spread * noise) if base else spread * noise
        out[name] = jnp.asarray(drawn.astype(out[name].dtype))
    for name, factor in factors.items():
        out[name] = (out[name] * factor).astype(out[name].dtype)
    return out
```

```python
import numpy as np
import concourse.bass as bass
from concourse import mybir

F32 = mybir.dt.float32
BF16 = mybir.dt.bfloat16
I32 = mybir.dt.int32
ALU = mybir.AluOpType
ACT = mybir.ActivationFunctionType
AX = mybir.AxisListType.X

P = 128
D = 128
J = 8
H = 2
JH = J // H
GE = P * J
W = 64
WW = 512
NT = 125
TC = 5
CN = NT * TC
EPS = 1e-5
CH = (19, 8)
SQ = ((4, 15), (4,))
RT = ((6, 17), (6,))


def program(nc, x, src, dst, ea, eps, We, be, W1, b1, bn_g, bn_b, bn_rm, bn_rv, W2, b2, ln_g, ln_b,
            Wm, Wself, out):
    N = x.shape[0]
    E = src.shape[0]
    G = -(-E // GE)
    PAIRS = G // 2
    assert G == 2 * PAIRS and N % (2 * CN) == 0
    DUP = G * GE - E
    CPAIRS = N // (2 * CN)
    NW = -(-N // WW)
    NPAD = NW * WW
    assert NPAD >= N + W

    x2_dram = nc.dram_tensor("x2_rows", (N, D), F32, kind="Internal").ap()

    from contextlib import ExitStack
    ctx = ExitStack()
    with ctx:
        def sb(name, shape, dt=F32):
            return ctx.enter_context(nc.sbuf_tensor(name, shape, dt))

        def ps(name, shape):
            return ctx.enter_context(nc.psum_tensor(name, shape, F32))

        def sem(name):
            return ctx.enter_context(nc.semaphore(name))

        acc = sb("acc", [P, NPAD])
        iota = sb("iota", [P, NPAD])
        ident = sb("ident", [P, P])
        keep = sb("keep", [P, J])
        keep1 = sb("keep1", [P, J])
        wrow = sb("wrow", [P, 3, D])
        WeT = sb("WeT", [P, D])
        W1T = sb("W1T", [P, D])
        W2T = sb("W2T", [P, D])
        Wm_sb = sb("Wm_sb", [P, D])
        Ws_sb = sb("Ws_sb", [P, D])
        cols = sb("cols", [P, 8])
        bn_scale = sb("bn_scale", [P, 1])
        bn_bias = sb("bn_bias", [P, 1])
        bn_t = sb("bn_t", [P, 4])
        one_eps = sb("one_eps", [P, 1])
        rows = sb("rows", [P, 3, D])
        be_row = sb("be_row", [1, 3, D])
        be_part = sb("be_part", [1, 3, D], BF16)
        be3 = sb("be3", [3, D], BF16)
        ones3 = sb("ones3", [3, P], BF16)

        ea_sb = [sb(f"ea{b}", [P, J, D]) for b in range(2)]
        srci = [sb(f"srci{b}", [P, J], I32) for b in range(2)]
        dsti = [sb(f"dsti{b}", [P, J], I32) for b in range(2)]
        xg = [sb(f"xg{b}", [P, J, D]) for b in range(2)]
        eaT = [sb(f"eaT{h}", [P, JH, P]) for h in range(H)]
        pre = [sb(f"pre{h}", [P, JH, D]) for h in range(H)]
        msg = [sb(f"msg{h}", [P, JH, D]) for h in range(H)]
        rel = sb("rel", [P, J])
        relm = sb("relm", [P, 2, J])
        hot = sb("hot", [P, J, W])
        vmax = sb("vmax", [P, J])
        vmin = sb("vmin", [P, J])
        viol = sb("viol", [P, 4])
        flag_f = sb("flag_f", [1, 2])
        flag = sb("flag", [1, 1], I32)
        dstf = sb("dstf", [P, 2, J])
        whot = sb("whot", [P, J, WW])

        xc = [sb(f"xc{b}", [NT, TC, D]) for b in range(2)]
        hT = sb("hT", [P, TC, NT])
        aT = sb("aT", [P, TC, NT])
        z = sb("z", [NT, 4, TC, D])
        st = sb("st", [NT, 12, TC])
        oc = [sb(f"oc{b}", [NT, TC, D]) for b in range(2)]

        psT2 = ps("psT", [P, J, P])
        psM2 = ps("psM", [P, J, D])
        psT = [psT2[:, h * JH:(h + 1) * JH, :] for h in range(H)]
        psM = [psM2[:, h * JH:(h + 1) * JH, :] for h in range(H)]
        psA = [ps(f"psA{b}", [P, WW]) for b in range(2)]
        psN = ps("psN", [P, 8, D])

        s_const = sem("s_const")
        s_ioc = sem("s_ioc")
        s_prep = sem("s_prep")
        s_wT = sem("s_wT")
        s_be = sem("s_be")
        s_bn = sem("s_bn")
        s_ready = sem("s_ready")
        s_ea = [sem(f"s_ea{b}") for b in range(2)]
        s_ix = [sem(f"s_ix{b}") for b in range(2)]
        s_xg = [sem(f"s_xg{b}") for b in range(2)]
        s_tr = [sem(f"s_tr{b}") for b in range(2)]
        s_eaT = sem("s_eaT")
        s_mm = sem("s_mm")
        s_pre = [sem(f"s_pre{b}") for b in range(2)]
        s_msg = sem("s_msg")
        s_ld = sem("s_ld")
        s_rel = sem("s_rel")
        s_hot = sem("s_hot")
        s_seg = sem("s_seg")
        s_acc = sem("s_acc")
        s_chk = sem("s_chk")
        s_chkp = sem("s_chkp")
        s_flag = sem("s_flag")
        g_in = [sem(f"g_in{l}") for l in range(2)]
        g_xg = [sem(f"g_xg{l}") for l in range(2)]
        g_tr = sem("g_tr")
        g_eaT = sem("g_eaT")
        g_mm = sem("g_mm")
        g_pre = sem("g_pre")
        g_msg = sem("g_msg")
        g_z = [sem(f"g_z{l}") for l in range(2)]
        g_df = [sem(f"g_df{l}") for l in range(2)]
        g_hot = [sem(f"g_hot{l}") for l in range(2)]
        g_seg = [sem(f"g_seg{l}") for l in range(2)]
        g_acc = [sem(f"g_acc{l}") for l in range(2)]
        t_ix = [sem(f"t_ix{b}") for b in range(2)]
        t_xg = [sem(f"t_xg{b}") for b in range(2)]
        t_ld = sem("t_ld")
        t_rel = sem("t_rel")
        t_hot = sem("t_hot")
        t_seg = [sem(f"t_seg{b}") for b in range(2)]
        t_acc = sem("t_acc")
        n_x = [[sem(f"n_x{l}{b}") for b in range(2)] for l in range(2)]
        n_xT = [sem(f"n_xT{l}") for l in range(2)]
        n_hT = [sem(f"n_hT{l}") for l in range(2)]
        n_h1 = sem("n_h1")
        n_a1 = sem("n_a1")
        n_h2 = [sem(f"n_h2{l}") for l in range(2)]
        n_ch = [sem(f"n_ch{l}") for l in range(2)]
        n_sq = [sem(f"n_sq{l}") for l in range(2)]
        n_aT = sem("n_aT")
        n_out = [[sem(f"n_out{l}{b}") for b in range(2)] for l in range(2)]
        s_through = sem("s_through")
        s_acc0 = sem("s_acc0")
        t_acc0 = sem("t_acc0")
        s_mask = sem("s_mask")
        t_mask = sem("t_mask")
        g_mask = [sem(f"g_mask{l}") for l in range(2)]
        s_done = [sem(f"s_done{l}") for l in range(2)]

        psT_node = psT2[:, 0:TC, 0:NT]
        psN_node = psN[:, 0:TC, 0:NT]
        psM_node = psM2[0:NT, 0:TC, :]

        block = ctx.enter_context(nc.Block())

        def later(value):
            return not isinstance(value, int) or value > 0

        def edges(t, off):
            return t[bass.ds(off, GE)].rearrange("(p j) -> p j", j=J)

        def attrs(off):
            return ea[bass.ds(off, GE), :].rearrange("(p j) d -> p (j d)", j=J)

        def group_offset(i, b, last):
            return E - GE if last and b == 1 else i * (2 * GE) + b * GE

        def node_rows(t, c):
            return t[bass.ds(c * CN, CN), :].rearrange("(t p) d -> p t d", p=NT)

        SMALL = 3 + 2 + 6 + 3 + 1

        @block.sync
        def _(sp):
            for k, w in enumerate((We, W1, W2)):
                sp.dma_start(wrow[:, k, :], w).then_inc(s_const, 16)
            sp.dma_start(Wm_sb[:, :], Wm).then_inc(s_const, 16)
            sp.dma_start(Ws_sb[:, :], Wself).then_inc(s_const, 16)
            for k, v in enumerate((b1, bn_g, bn_b, bn_rm, bn_rv)):
                sp.dma_start(cols[:, k:k + 1], v.rearrange("(p o) -> p o", o=1)).then_inc(s_const, 16)
            sp.dma_start(cols[:, 5:6], eps.rearrange("(a o) -> a o", o=1).broadcast_to([P, 1])).then_inc(s_const, 16)
            for k, v in enumerate((b2, ln_g, ln_b)):
                sp.dma_start(rows[:, k, :], v.rearrange("(o d) -> o d", o=1).broadcast_to([P, D])).then_inc(s_const, 16)
            sp.dma_start(be_row[:, 0, :], be.rearrange("(o d) -> o d", o=1)).then_inc(s_const, 16)
            sp.wait_ge(s_prep, 5)
            for k in range(3):
                sp.dma_start(be3[k:k + 1, :], be_part[0:1, k, :]).then_inc(s_be, 16)

            def load(i, b, last):
                off = group_offset(i, b, last)
                if later(16 * J * i):
                    sp.wait_ge(s_xg[b], 16 * J * i)
                sp.sem_inc(s_through, 1)
                if later(2 * i):
                    sp.wait_ge(s_acc, 2 * i)
                sp.dma_start(srci[b][:, :], edges(src, off)).then_inc(s_ix[b], 16)
                sp.dma_start(dsti[b][:, :], edges(dst, off)).then_inc(s_ea[b], 16)
                if later(H * i):
                    sp.wait_ge(s_tr[b], H * i)
                sp.dma_start(ea_sb[b][:, :, :].rearrange("p j d -> p (j d)"), attrs(off)).then_inc(s_ea[b], 16)

            for b in range(2):
                load(0, b, False)
            with sp.Fori(1, PAIRS - 1) as i:
                for b in range(2):
                    load(i, b, False)
            for b in range(2):
                load(PAIRS - 1, b, True)

            def general_loads(l, sp_off, g):
                if later(g * NW):
                    sp.wait_ge(g_acc[l], g * NW)
                sp.dma_start(srci[0][:, :], edges(src, sp_off)).then_inc(g_in[l], 16)
                sp.dma_start(dsti[0][:, :], edges(dst, sp_off)).then_inc(g_in[l], 16)
                if l == 0:
                    sp.dma_start(ea_sb[0][:, :, :].rearrange("p j d -> p (j d)"), attrs(sp_off)).then_inc(g_in[l], 16)

            def general(l):
                sp.wait_ge(s_flag, 1)
                v = sp.value_load(flag[0:1, 0:1], min_val=0, max_val=1)
                with sp.If(v == 1):
                    general_loads(l, 0, 0)
                    with sp.Fori(1, G - 1) as g:
                        general_loads(l, g * GE, g)
                    general_loads(l, E - GE, G - 1)

            general(0)

            def nodes(l, source, target):
                sp.wait_ge(s_done[l], 1)
                def step(i):
                    for b in range(2):
                        c = i * 2 + b
                        if later(16 * i):
                            sp.wait_ge(n_out[l][b], 16 * i)
                        sp.dma_start(xc[b][:, :, :], node_rows(source, c)).then_inc(n_x[l][b], 16)
                    for b in range(2):
                        c = i * 2 + b
                        sp.wait_ge(n_ch[l], c * CH[l] + CH[l])
                        sp.dma_start(node_rows(target, c), oc[b][:, :, :]).then_inc(n_out[l][b], 16)

                step(0)
                with sp.Fori(1, CPAIRS) as i:
                    step(i)

                for b in range(2):
                    sp.wait_ge(n_out[l][b], 16 * CPAIRS)

            nodes(0, x, x2_dram)

            def load2(i, b, last):
                off = group_offset(i, b, last)
                if later(16 * J * i):
                    sp.wait_ge(t_xg[b], 16 * J * i)
                sp.sem_inc(s_through, 1)
                if later(2 * i):
                    sp.wait_ge(t_acc, 2 * i)
                sp.dma_start(srci[b][:, :], edges(src, off)).then_inc(t_ix[b], 16)
                sp.dma_start(dsti[b][:, :], edges(dst, off)).then_inc(t_ix[b], 16)

            for b in range(2):
                load2(0, b, False)
            with sp.Fori(1, PAIRS - 1) as i:
                for b in range(2):
                    load2(i, b, False)
            for b in range(2):
                load2(PAIRS - 1, b, True)
            general(1)
            nodes(1, x2_dram, out)

        @block.gpsimd
        def _(pool):
            pool.memset(ident[:, :], 0.0).then_inc(s_ioc, 1)
            pool.memset(keep[:, :], 1.0).then_inc(s_ioc, 1)
            pool.memset(ones3[:, :], 1.0).then_inc(s_ioc, 1)
            pool.wait_ge(s_ioc, 3)
            pool.affine_select(out=ident[:, :], in_=ident[:, :], compare_op=ALU.not_equal, fill=1.0, base=0,
                               pattern=[[-1, P]], channel_multiplier=1).then_inc(s_ioc, 1)
            pool.affine_select(out=keep[:, :], in_=keep[:, :], compare_op=ALU.is_ge, fill=0.0, base=-DUP,
                               pattern=[[1, J]], channel_multiplier=J).then_inc(s_ioc, 1)
            pool.iota(iota[:, :], [[1, NPAD]], base=0, channel_multiplier=0,
                      allow_small_or_imprecise_dtypes=True).then_inc(s_ioc, 1)

            def gather(table, idx, rows_, signal):
                pool.sem_inc(s_through, 1)
                for j in range(J):
                    pool.indirect_dma_start(rows_[:, j, :], None, table,
                                            bass.IndirectOffsetOnAxis(ap=idx[:, j:j + 1], axis=0)).then_inc(signal, 16)

            def group(i, b):
                pool.wait_ge(s_ix[b], 16 * i + 16)
                if later(H * i):
                    pool.wait_ge(s_pre[b], H * i)
                gather(x[:, :], srci[b], xg[b], s_xg[b])

            for b in range(2):
                group(0, b)
            with pool.Fori(1, PAIRS) as i:
                for b in range(2):
                    group(i, b)

            def general(l, table):
                pool.wait_ge(s_flag, 1)
                v = pool.value_load(flag[0:1, 0:1], min_val=0, max_val=1)
                with pool.If(v == 1):
                    def group(g):
                        pool.wait_ge(g_in[l], g * (48 - 16 * l) + (48 - 16 * l))
                        if later(g * NW):
                            pool.wait_ge(g_acc[l], g * NW)
                        gather(table, srci[0], xg[0], g_xg[l])

                    group(0)
                    with pool.Fori(1, G) as g:
                        group(g)

            general(0, x[:, :])
            for b in range(2):
                pool.wait_ge(n_out[0][b], 16 * CPAIRS)

            def group2(i, b):
                pool.wait_ge(t_ix[b], 32 * i + 32)
                if later(i):
                    pool.wait_ge(t_seg[b], i)
                gather(x2_dram[:, :], srci[b], xg[b], t_xg[b])

            for b in range(2):
                group2(0, b)
            with pool.Fori(1, PAIRS) as i:
                for b in range(2):
                    group2(i, b)
            general(1, x2_dram[:, :])

        @block.scalar
        def _(act):
            act.wait_ge(s_prep, 7)
            nc.scalar.activation(bn_t[:, 1:2], bn_t[:, 0:1], ACT.Sqrt).then_inc(s_bn, 1)

            def group(i, b):
                for h in range(H):
                    act.wait_ge(s_tr[b], H * i + h + 1)
                    if later(4 * i + 2 * b):
                        act.wait_ge(s_mm, 4 * i + 2 * b)
                    nc.scalar.copy(eaT[h][:, :, :], psT[h][:, :, :]).then_inc(s_eaT, 1)
                for h in range(H):
                    act.wait_ge(s_pre[b], H * i + h + 1)
                    if later(2 * i + b):
                        act.wait_ge(s_seg, 2 * i + b)
                    nc.scalar.activation(msg[h][:, :, :], pre[h][:, :, :], ACT.Relu).then_inc(s_msg, 1)

            for b in range(2):
                group(0, b)
            with act.Fori(1, PAIRS) as i:
                for b in range(2):
                    group(i, b)

            act.wait_ge(s_flag, 1)
            v = act.value_load(flag[0:1, 0:1], min_val=0, max_val=1)
            with act.If(v == 1):
                def general_group(g):
                    for h in range(H):
                        act.wait_ge(g_tr, g * H + (h + 1))
                        if later(g * H):
                            act.wait_ge(g_mm, g * H)
                        nc.scalar.copy(eaT[h][:, :, :], psT[h][:, :, :]).then_inc(g_eaT, 1)
                    for h in range(H):
                        act.wait_ge(g_pre, g * H + (h + 1))
                        if later(g * NW):
                            act.wait_ge(g_seg[0], g * NW)
                        nc.scalar.activation(msg[h][:, :, :], pre[h][:, :, :], ACT.Relu).then_inc(g_msg, 1)

                general_group(0)
                with act.Fori(1, G) as g:
                    general_group(g)

            def step(c):
                act.wait_ge(n_h1, c + 1)
                if later(c):
                    act.wait_ge(n_h2[0], c)
                nc.scalar.activation(aT[:, :, :], psT_node, ACT.Relu, bias=bn_bias[:, :],
                                     scale=bn_scale[:, :]).then_inc(n_a1, 1)
                for k in range(2):
                    act.wait_ge(n_ch[0], c * CH[0] + SQ[0][k])
                    nc.scalar.activation(z[:, 1, :, :], z[:, 0, :, :], ACT.Square).then_inc(n_sq[0], 1)
                    act.wait_ge(n_ch[0], c * CH[0] + RT[0][k])
                    nc.scalar.activation(st[:, 4, :], st[:, 3, :], ACT.Sqrt).then_inc(n_sq[0], 1)

            step(0)
            with act.Fori(1, 2 * CPAIRS) as c:
                step(c)

            def step(c):
                act.wait_ge(n_xT[1], c + 1)
                if later(c):
                    act.wait_ge(n_h2[1], c)
                nc.scalar.copy(aT[:, :, :], psN_node).then_inc(n_aT, 1)
                act.wait_ge(n_ch[1], c * CH[1] + SQ[1][0])
                nc.scalar.activation(z[:, 1, :, :], z[:, 0, :, :], ACT.Square).then_inc(n_sq[1], 1)
                act.wait_ge(n_ch[1], c * CH[1] + RT[1][0])
                nc.scalar.activation(st[:, 4, :], st[:, 3, :], ACT.Sqrt).then_inc(n_sq[1], 1)

            step(0)
            with act.Fori(1, 2 * CPAIRS) as c:
                step(c)

        @block.vector
        def _(dve):
            nc.vector.memset(acc[:, :], 0.0).then_inc(s_acc0, 1)
            nc.vector.memset(vmax[:, :], 0.0).then_inc(s_acc0, 1)
            nc.vector.memset(vmin[:, :], 0.0).then_inc(s_acc0, 1)
            dve.wait_ge(s_const, 16 * SMALL)
            n = [0]

            def prep(ins):
                n[0] += 1
                ins.then_inc(s_prep, 1)
                dve.wait_ge(s_prep, n[0])

            prep(nc.vector.tensor_copy(be_part[:, 0, :], be_row[:, 0, :]))
            prep(nc.vector.tensor_sub(be_row[:, 1, :], be_row[:, 0, :], be_part[:, 0, :]))
            prep(nc.vector.tensor_copy(be_part[:, 1, :], be_row[:, 1, :]))
            prep(nc.vector.tensor_sub(be_row[:, 2, :], be_row[:, 1, :], be_part[:, 1, :]))
            prep(nc.vector.tensor_copy(be_part[:, 2, :], be_row[:, 2, :]))
            prep(nc.vector.tensor_scalar(one_eps[:, :], cols[:, 5:6], 1.0, None, ALU.add))
            prep(nc.vector.tensor_scalar(bn_t[:, 0:1], cols[:, 4:5], EPS, None, ALU.add))
            dve.wait_ge(s_bn, 1)
            prep(nc.vector.reciprocal(bn_t[:, 2:3], bn_t[:, 1:2]))
            prep(nc.vector.tensor_mul(bn_scale[:, :], bn_t[:, 2:3], cols[:, 1:2]))
            prep(nc.vector.tensor_sub(bn_t[:, 3:4], cols[:, 0:1], cols[:, 3:4]))
            prep(nc.vector.scalar_tensor_tensor(out=bn_bias[:, :], in0=bn_t[:, 3:4], scalar=bn_scale[:, :],
                                                in1=cols[:, 2:3], op0=ALU.mult, op1=ALU.add))
            dve.wait_ge(s_ioc, 6)
            prep(nc.vector.tensor_scalar(keep1[:, :], keep[:, :], -1.0, None, ALU.add))
            dve.wait_ge(s_wT, 1)
            for k, t in enumerate((WeT, W1T, W2T)):
                nc.vector.tensor_copy(t[:, :], psT[0][:, k, :]).then_inc(s_ready, 1)
            dve.wait_ge(s_acc0, 3)

            hot_in1 = iota[:, 0:W].unsqueeze(1).broadcast_to([P, J, W])

            def base_of(idx):
                dve.sem_inc(s_through, 1)
                return dve.value_load(idx[0:1, 0:1], min_val=0, max_val=N - 1)

            def masked(where, signal):
                nc.vector.tensor_mul(relm[:, 0, :], where, keep[:, :]).then_inc(signal, 1)
                dve.wait_ge(signal, 1)
                nc.vector.tensor_add(relm[:, 1, :], relm[:, 0, :], keep1[:, :]).then_inc(signal, 1)
                dve.wait_ge(signal, 2)
                return relm[:, 1, :]

            def group(i, b, last):
                g = i * 2 + b
                dve.wait_ge(s_ea[b], 32 * i + 32)
                base = base_of(dsti[b])
                if later(g):
                    dve.wait_ge(s_hot, g)
                nc.vector.tensor_scalar(rel[:, :], dsti[b][:, :], iota[:, bass.ds(base, 1)], None,
                                        ALU.subtract).then_inc(s_rel, 1)
                dve.wait_ge(s_rel, g * 3 + 1)
                nc.vector.tensor_tensor(vmax[:, :], vmax[:, :], rel[:, :], ALU.max).then_inc(s_rel, 1)
                nc.vector.tensor_tensor(vmin[:, :], vmin[:, :], rel[:, :], ALU.min).then_inc(s_rel, 1)
                dve.wait_ge(s_rel, g * 3 + 3)
                where = masked(rel[:, :], s_mask) if last and b == 1 else rel[:, :]
                if later(g):
                    dve.wait_ge(s_seg, g)
                nc.vector.tensor_tensor(hot[:, :, :], where.unsqueeze(2).broadcast_to([P, J, W]), hot_in1,
                                        ALU.is_equal).then_inc(s_hot, 1)
                dve.wait_ge(s_xg[b], 16 * J * i + 16 * J)
                if later(2 * g):
                    dve.wait_ge(s_msg, 2 * g)
                for h in range(H):
                    dve.wait_ge(s_mm, g * 2 + (h + 1))
                    nc.vector.tensor_add(pre[h][:, :, :], psM[h][:, :, :],
                                         xg[b][:, h * JH:(h + 1) * JH, :]).then_inc(s_pre[b], 1)
                dve.wait_ge(s_seg, g + 1)
                if later(g):
                    dve.wait_ge(s_acc, g)
                nc.vector.tensor_add(acc[:, bass.ds(base, W)], acc[:, bass.ds(base, W)],
                                     psA[0][:, 0:W]).then_inc(s_acc, 1)

            for b in range(2):
                group(0, b, False)
            with dve.Fori(1, PAIRS - 1) as i:
                for b in range(2):
                    group(i, b, False)
            for b in range(2):
                group(PAIRS - 1, b, True)

            k = [0]

            def chk(ins):
                k[0] += 1
                ins.then_inc(s_chk, 1)
                dve.wait_ge(s_chk, k[0])

            chk(nc.vector.tensor_reduce(viol[:, 0:1], vmax[:, :], axis=AX, op=ALU.max))
            chk(nc.vector.tensor_reduce(viol[:, 1:2], vmin[:, :], axis=AX, op=ALU.min))
            chk(nc.vector.tensor_scalar(viol[:, 2:3], viol[:, 0:1], float(-(W - 1)), None, ALU.add))
            chk(nc.vector.tensor_scalar(viol[:, 3:4], viol[:, 1:2], -1.0, None, ALU.mult))
            chk(nc.vector.tensor_max(viol[:, 0:1], viol[:, 2:3], viol[:, 3:4]))
            dve.wait_ge(s_chkp, 1)
            chk(nc.vector.tensor_reduce(flag_f[:, 0:1], psA[1][0:1, 0:P], axis=AX, op=ALU.max))
            nc.vector.tensor_scalar(flag[:, :], flag_f[:, 0:1], 0.0, None, ALU.is_gt).then_inc(s_flag, 1)

            def general_group(l, g, last):
                dve.wait_ge(g_in[l], g * (48 - 16 * l) + (48 - 16 * l))
                if later(g * NW):
                    dve.wait_ge(g_acc[l], g * NW)
                nc.vector.tensor_copy(dstf[:, 0, :], dsti[0][:, :]).then_inc(g_df[l], 1)
                dve.wait_ge(g_df[l], g + 1)
                where = masked(dstf[:, 0, :], g_mask[l]) if last else dstf[:, 0, :]
                if l == 0:
                    dve.wait_ge(g_xg[l], g * (16 * J) + 16 * J)
                    if later(g * H):
                        dve.wait_ge(g_msg, g * H)
                    for h in range(H):
                        dve.wait_ge(g_mm, g * H + (h + 1))
                        nc.vector.tensor_add(pre[h][:, :, :], psM[h][:, :, :],
                                             xg[0][:, h * JH:(h + 1) * JH, :]).then_inc(g_pre, 1)
                dve.sem_inc(s_through, 1)
                with dve.Fori(0, NW) as w:
                    nc.vector.tensor_tensor(whot[:, :, :], where.unsqueeze(2).broadcast_to([P, J, WW]),
                                            iota[:, bass.ds(w * WW, WW)].unsqueeze(1).broadcast_to([P, J, WW]),
                                            ALU.is_equal).then_inc(g_hot[l], 1)
                    dve.wait_ge(g_seg[l], g * NW + w + 1)
                    nc.vector.tensor_add(acc[:, bass.ds(w * WW, WW)], acc[:, bass.ds(w * WW, WW)],
                                         psA[0][:, :]).then_inc(g_acc[l], 1)
                    dve.wait_ge(g_acc[l], g * NW + w + 1)

            def general(l):
                dve.wait_ge(s_flag, 1)
                v = dve.value_load(flag[0:1, 0:1], min_val=0, max_val=1)
                with dve.If(v == 1):
                    nc.vector.memset(acc[:, :], 0.0).then_inc(g_z[l], 1)
                    dve.wait_ge(g_z[l], 1)
                    general_group(l, 0, False)
                    with dve.Fori(1, G - 1) as g:
                        general_group(l, g, False)
                    general_group(l, G - 1, True)
                    dve.wait_ge(g_acc[l], G * NW)

            dve.wait_ge(s_acc, G)
            general(0)
            nc.vector.memset(st[:, 11, :], 0.0).then_inc(s_done[0], 1)

            def chain(l, c):
                k = [0]

                def link(ins):
                    k[0] += 1
                    ins.then_inc(n_ch[l], 1)
                    dve.wait_ge(n_ch[l], c * CH[l] + k[0])
                    return k[0]
                return link

            def per_row(col):
                return st[:, col, :].unsqueeze(2).broadcast_to([NT, TC, D])

            def norm(l, c, link, slot, which, result):
                link(nc.vector.tensor_reduce(st[:, 0, :], z[:, slot, :, :], axis=AX, op=ALU.add))
                link(nc.vector.tensor_scalar(st[:, 1, :], st[:, 0, :], 1.0 / D, None, ALU.mult))
                at = link(nc.vector.tensor_sub(z[:, 0, :, :], z[:, slot, :, :], per_row(1)))
                assert at == SQ[l][which], at
                dve.wait_ge(n_sq[l], c * (2 * len(SQ[l])) + 2 * which + 1)
                link(nc.vector.tensor_reduce(st[:, 2, :], z[:, 1, :, :], axis=AX, op=ALU.add))
                at = link(nc.vector.tensor_scalar(st[:, 3, :], st[:, 2, :], 1.0 / D, EPS, ALU.mult, ALU.add))
                assert at == RT[l][which], at
                dve.wait_ge(n_sq[l], c * (2 * len(SQ[l])) + 2 * which + 2)
                link(nc.vector.reciprocal(st[:, 5, :], st[:, 4, :]))
                link(nc.vector.tensor_mul(result, z[:, 0, :, :], per_row(5)))

            def param(k):
                return rows[0:NT, k, :].unsqueeze(1).broadcast_to([NT, TC, D])

            def step(i):
                for b in range(2):
                    c = i * 2 + b
                    link = chain(0, c)
                    dve.wait_ge(n_xT[0], c + 1)
                    if later(c):
                        dve.wait_ge(n_h1, c)
                    nc.vector.scalar_tensor_tensor(
                        out=hT[:, :, :], in0=psN_node, scalar=one_eps[:, :],
                        in1=acc[:, bass.ds(c * CN, CN)].rearrange("d (t n) -> d t n", t=TC),
                        op0=ALU.mult, op1=ALU.add).then_inc(n_hT[0], 1)
                    dve.wait_ge(n_h2[0], c + 1)
                    if later(c * CH[0]):
                        dve.wait_ge(n_ch[0], c * CH[0])
                    link(nc.vector.tensor_add(z[:, 2, :, :], psM_node, param(0)))
                    norm(0, c, link, 2, 0, z[:, 3, :, :])
                    link(nc.vector.tensor_mul(z[:, 2, :, :], z[:, 3, :, :], param(1)))
                    link(nc.vector.tensor_add(z[:, 3, :, :], z[:, 2, :, :], param(2)))
                    link(nc.vector.tensor_add(z[:, 2, :, :], z[:, 3, :, :], xc[b][:, :, :]))
                    link(nc.vector.scalar_tensor_tensor(out=z[:, 3, :, :], in0=z[:, 2, :, :], scalar=0.0,
                                                        in1=xc[b][:, :, :], op0=ALU.max, op1=ALU.add))
                    if later(16 * i):
                        dve.wait_ge(n_out[0][b], 16 * i)
                    norm(0, c, link, 3, 1, oc[b][:, :, :])

            step(0)
            with dve.Fori(1, CPAIRS) as i:
                step(i)

            nc.vector.memset(acc[:, :], 0.0).then_inc(t_acc0, 1)
            dve.wait_ge(t_acc0, 1)

            def group2(i, b, last):
                g = i * 2 + b
                dve.wait_ge(t_ix[b], 32 * i + 32)
                base = base_of(dsti[b])
                if later(g):
                    dve.wait_ge(t_hot, g)
                nc.vector.tensor_scalar(rel[:, :], dsti[b][:, :], iota[:, bass.ds(base, 1)], None,
                                        ALU.subtract).then_inc(t_rel, 1)
                dve.wait_ge(t_rel, g + 1)
                where = masked(rel[:, :], t_mask) if last and b == 1 else rel[:, :]
                for bb, n_ in ((0, i + 1 if b else i), (1, i)):
                    if later(n_):
                        dve.wait_ge(t_seg[bb], n_)
                nc.vector.tensor_tensor(hot[:, :, :], where.unsqueeze(2).broadcast_to([P, J, W]), hot_in1,
                                        ALU.is_equal).then_inc(t_hot, 1)
                dve.wait_ge(t_seg[b], i + 1)
                if later(g):
                    dve.wait_ge(t_acc, g)
                nc.vector.tensor_add(acc[:, bass.ds(base, W)], acc[:, bass.ds(base, W)],
                                     psA[0][:, 0:W]).then_inc(t_acc, 1)

            for b in range(2):
                group2(0, b, False)
            with dve.Fori(1, PAIRS - 1) as i:
                for b in range(2):
                    group2(i, b, False)
            for b in range(2):
                group2(PAIRS - 1, b, True)
            dve.wait_ge(t_acc, G)
            general(1)
            nc.vector.memset(st[:, 11, :], 0.0).then_inc(s_done[1], 1)

            def step(i):
                for b in range(2):
                    c = i * 2 + b
                    link = chain(1, c)
                    if later(c):
                        dve.wait_ge(n_h2[1], c)
                    nc.vector.tensor_copy(hT[:, :, :], acc[:, bass.ds(c * CN, CN)].rearrange(
                        "d (t n) -> d t n", t=TC)).then_inc(n_hT[1], 1)
                    dve.wait_ge(n_h2[1], c + 1)
                    if later(c * CH[1]):
                        dve.wait_ge(n_ch[1], c * CH[1])
                    link(nc.vector.tensor_add(z[:, 2, :, :], psM_node, xc[b][:, :, :]))
                    if later(16 * i):
                        dve.wait_ge(n_out[1][b], 16 * i)
                    norm(1, c, link, 2, 0, oc[b][:, :, :])

            step(0)
            with dve.Fori(1, CPAIRS) as i:
                step(i)

        @block.tensor
        def _(pe):
            pe.wait_ge(s_const, 16 * SMALL)
            pe.wait_ge(s_ioc, 6)
            for k in range(3):
                last_ = nc.tensor.transpose(psT[0][:, k, :], wrow[:, k, :], ident[:, :])
            last_.then_inc(s_wT, 1)
            pe.wait_ge(s_ready, 3)
            pe.wait_ge(s_be, 48)

            def transpose_group(b, signal):
                for h in range(H):
                    for j in range(JH):
                        ins = nc.tensor.transpose(psT[h][:, j, :], ea_sb[b][:, h * JH + j, :], ident[:, :])
                    ins.then_inc(signal, 1)

            def project(h, signal):
                nc.tensor.matmul(psM[h][:, :, :], ones3[:, :], be3[:, :].unsqueeze(1).broadcast_to([3, JH, D]),
                                 start=True, stop=False)
                for j in range(JH):
                    ins = nc.tensor.matmul(psM[h][:, j, :], eaT[h][:, j, :], WeT[:, :], start=False,
                                           stop=j == JH - 1)
                ins.then_inc(signal, 1)

            def group(i, b):
                g = i * 2 + b
                pe.wait_ge(s_ea[b], 32 * i + 32)
                if later(2 * g):
                    pe.wait_ge(s_eaT, 2 * g)
                transpose_group(b, s_tr[b])
                if later(H * (i + b)):
                    pe.wait_ge(s_pre[1 - b], H * (i + b))
                for h in range(H):
                    pe.wait_ge(s_eaT, g * 2 + (h + 1))
                    project(h, s_mm)
                pe.wait_ge(s_hot, g + 1)
                if later(g):
                    pe.wait_ge(s_acc, g)
                for h in range(H):
                    pe.wait_ge(s_msg, g * 2 + (h + 1))
                    for j in range(JH):
                        ins = nc.tensor.matmul(psA[0][:, 0:W], msg[h][:, j, :], hot[:, h * JH + j, :],
                                               start=h + j == 0, stop=h * JH + j == J - 1)
                ins.then_inc(s_seg, 1)

            for b in range(2):
                group(0, b)
            with pe.Fori(1, PAIRS) as i:
                for b in range(2):
                    group(i, b)

            pe.wait_ge(s_chk, 5)
            nc.tensor.matmul(psA[1][0:1, 0:P], viol[:, 0:1], ident[:, :], start=True, stop=True).then_inc(s_chkp, 1)

            def general(l):
                pe.wait_ge(s_flag, 1)
                v = pe.value_load(flag[0:1, 0:1], min_val=0, max_val=1)
                with pe.If(v == 1):
                    def group(g):
                        if l == 0:
                            pe.wait_ge(g_in[l], g * 48 + 48)
                            if later(g * H):
                                pe.wait_ge(g_eaT, g * H)
                            transpose_group(0, g_tr)
                            if later(g * H):
                                pe.wait_ge(g_pre, g * H)
                            for h in range(H):
                                pe.wait_ge(g_eaT, g * H + (h + 1))
                                project(h, g_mm)
                            pe.wait_ge(g_msg, g * H + H)
                        else:
                            pe.wait_ge(g_xg[l], g * (16 * J) + 16 * J)
                        pe.sem_inc(s_through, 1)
                        with pe.Fori(0, NW) as w:
                            pe.wait_ge(g_hot[l], g * NW + w + 1)
                            for j in range(J):
                                rows_ = msg[j // JH][:, j % JH, :] if l == 0 else xg[0][:, j, :]
                                ins = nc.tensor.matmul(psA[0][:, :], rows_, whot[:, j, :], start=j == 0,
                                                       stop=j == J - 1)
                            ins.then_inc(g_seg[l], 1)

                    group(0)
                    with pe.Fori(1, G) as g:
                        group(g)

            general(0)

            def step(i):
                for b in range(2):
                    c = i * 2 + b
                    pe.wait_ge(n_x[0][b], 16 * i + 16)
                    if later(c):
                        pe.wait_ge(n_hT[0], c)
                    for t in range(TC):
                        ins = nc.tensor.transpose(psN[:, t, 0:NT], xc[b][:, t, :], ident[0:NT, 0:NT])
                    ins.then_inc(n_xT[0], 1)
                    pe.wait_ge(n_hT[0], c + 1)
                    if later(c):
                        pe.wait_ge(n_a1, c)
                    for t in range(TC):
                        ins = nc.tensor.matmul(psT2[:, t, 0:NT], W1T[:, :], hT[:, t, :], start=True, stop=True)
                    ins.then_inc(n_h1, 1)
                    pe.wait_ge(n_a1, c + 1)
                    if later(c * CH[0]):
                        pe.wait_ge(n_ch[0], c * CH[0])
                    for t in range(TC):
                        ins = nc.tensor.matmul(psM2[0:NT, t, :], aT[:, t, :], W2T[:, :], start=True, stop=True)
                    ins.then_inc(n_h2[0], 1)

            step(0)
            with pe.Fori(1, CPAIRS) as i:
                step(i)

            def group2(i, b):
                g = i * 2 + b
                pe.wait_ge(t_hot, g + 1)
                pe.wait_ge(t_xg[b], 16 * J * i + 16 * J)
                if later(g):
                    pe.wait_ge(t_acc, g)
                for j in range(J):
                    ins = nc.tensor.matmul(psA[0][:, 0:W], xg[b][:, j, :], hot[:, j, :], start=j == 0,
                                           stop=j == J - 1)
                ins.then_inc(t_seg[b], 1)

            for b in range(2):
                group2(0, b)
            with pe.Fori(1, PAIRS) as i:
                for b in range(2):
                    group2(i, b)
            general(1)

            def step(i):
                for b in range(2):
                    c = i * 2 + b
                    pe.wait_ge(n_x[1][b], 16 * i + 16)
                    if later(c):
                        pe.wait_ge(n_aT, c)
                    for t in range(TC):
                        ins = nc.tensor.transpose(psN[:, t, 0:NT], xc[b][:, t, :], ident[0:NT, 0:NT])
                    ins.then_inc(n_xT[1], 1)
                    pe.wait_ge(n_hT[1], c + 1)
                    pe.wait_ge(n_aT, c + 1)
                    if later(c * CH[1]):
                        pe.wait_ge(n_ch[1], c * CH[1])
                    for t in range(TC):
                        nc.tensor.matmul(psM2[0:NT, t, :], hT[:, t, :], Wm_sb[:, :], start=True, stop=False)
                        ins = nc.tensor.matmul(psM2[0:NT, t, :], aT[:, t, :], Ws_sb[:, :], start=False, stop=True)
                    ins.then_inc(n_h2[1], 1)

            step(0)
            with pe.Fori(1, CPAIRS) as i:
                step(i)

_INS = ["x", "src", "dst", "edge_attr_128", "L0_gnn_eps", "L0_gnn_We", "L0_gnn_be", "L0_gnn_W1", "L0_gnn_b1",
        "L0_gnn_bn_g", "L0_gnn_bn_b", "L0_gnn_bn_rm", "L0_gnn_bn_rv", "L0_gnn_W2", "L0_gnn_b2", "L0_gnn_ln_g",
        "L0_gnn_ln_b", "L1_gnn_W", "L1_gnn_W_self"]


def kernel(**inputs):
    import concourse.bacc as bacc
    from concourse.bass_utils import run_bass_kernel_spmd

    nc = bacc.Bacc("TRN2", target_bir_lowering=False, num_devices=1)
    arrays, args = {}, []
    for name in _INS:
        a = np.ascontiguousarray(inputs[name])
        if a.ndim == 0:
            a = a.reshape(1)
        arrays[f"in_{name}"] = a
        args.append(nc.dram_tensor(f"in_{name}", a.shape, mybir.dt.from_np(a.dtype), kind="ExternalInput").ap())
    n = inputs["x"].shape[0]
    out = nc.dram_tensor("out_rows", (n, D), F32, kind="ExternalOutput").ap()
    program(nc, *args, out)
    r = run_bass_kernel_spmd(nc, [arrays], core_ids=[0])
    return r.results[0]["out_rows"]
```

```python
import numpy as np
import concourse.bass as bass
from concourse import mybir

F32 = mybir.dt.float32
BF16 = mybir.dt.bfloat16
F16 = mybir.dt.float16
I32 = mybir.dt.int32
ALU = mybir.AluOpType
ACT = mybir.ActivationFunctionType
AX = mybir.AxisListType.X

P = 128
D = 128
J = 8
H = 2
JH = J // H
GE = P * J
W = 40
WW = 512
NT = 125
TC = 5
CN = NT * TC
QN = 8
QT = 4
QG = 4
HN = 50
CB = HN * QN
GW = QG * QN
DG = 10
HP = 10
NP_ = HN // HP
ROUND = 12582912.0
EPS = 1e-5
CH = (19, 8)
SQ = ((4, 15), (4,))
RT = ((6, 17), (6,))


def program(nc, x, src, dst, ea, eps, We, be, W1, b1, bn_g, bn_b, bn_rm, bn_rv, W2, b2, ln_g, ln_b,
            Wm, Wself, out):
    N = x.shape[0]
    E = src.shape[0]
    G = -(-E // GE)
    PAIRS = G // 2
    assert G == 2 * PAIRS and N % (2 * CN) == 0
    DUP = G * GE - E
    CPAIRS = N // (2 * CN)
    NW = -(-N // WW)
    NPAD = NW * WW
    assert NPAD >= N + W
    KT = E // P
    KREM = E - KT * P
    KC = -(-(KT + 1) // P)
    KPAD = KC * P
    KFULL = KT // P
    NQ = QG * G
    DC = 10
    assert HN * NT == N and DC * CN == N and DC * 2 * DG * GW >= N and NQ * QN >= N and KREM > 0

    x2_dram = nc.dram_tensor("x2_rows", (N, D), F32, kind="Internal").ap()

    counts = nc.dram_tensor("counts", (G, P, HN * GW), F16, kind="Internal").ap()

    from contextlib import ExitStack
    ctx = ExitStack()
    with ctx:
        def sb(name, shape, dt=F32):
            return ctx.enter_context(nc.sbuf_tensor(name, shape, dt))

        def ps(name, shape):
            return ctx.enter_context(nc.psum_tensor(name, shape, F32))

        def sem(name):
            return ctx.enter_context(nc.semaphore(name))

        acc = sb("acc", [P, NPAD])
        iota = sb("iota", [P, NPAD])
        ident = sb("ident", [P, P])
        keep = sb("keep", [P, J])
        keep1 = sb("keep1", [P, J])
        wrow = sb("wrow", [P, 3, D])
        WeT = sb("WeT", [P, D])
        W1T = sb("W1T", [P, D])
        W2T = sb("W2T", [P, D])
        Wm_sb = sb("Wm_sb", [P, D])
        Ws_sb = sb("Ws_sb", [P, D])
        cols = sb("cols", [P, 8])
        bn_scale = sb("bn_scale", [P, 1])
        bn_bias = sb("bn_bias", [P, 1])
        bn_t = sb("bn_t", [P, 4])
        one_eps = sb("one_eps", [P, 1])
        rows = sb("rows", [P, 3, D])
        be_row = sb("be_row", [1, 3, D])
        be_part = sb("be_part", [1, 3, D], BF16)
        be3 = sb("be3", [3, D], BF16)
        ones3 = sb("ones3", [3, P], BF16)

        reg = sb("reg", [P, 5760])
        Rh = [reg[:, n * 800:(n + 1) * 800].bitcast(BF16).rearrange("p (t c) -> p t c", t=QT) for n in range(2)]
        cbuf = [reg[:, 1600 + b * 800:2400 + b * 800].bitcast(F16).rearrange("p (t n) -> p t n", t=HN)
                for b in range(2)]
        Lh = [reg[:, 3200 + n * 256:3456 + n * 256].bitcast(BF16).rearrange("p (t c) -> p t c", t=QT)
              for n in range(2)]
        ea_sb = [reg[:, 3712 + b * 1024:4736 + b * 1024].rearrange("p (j d) -> p j d", j=J) for b in range(2)]
        z = reg[0:NT, 0:2560].rearrange("p (s t d) -> p s t d", s=4, t=TC)
        rest = reg[0:NT, 2560:3840].rearrange("p (s t d) -> p s t d", s=2, t=TC)
        hT = reg[:, 3840:4465].rearrange("p (t n) -> p t n", t=TC)
        aT = reg[:, 4480:5105].rearrange("p (t n) -> p t n", t=TC)
        srci = [sb(f"srci{b}", [P, J], I32) for b in range(2)]
        dsti = [sb(f"dsti{b}", [P, J], I32) for b in range(2)]
        xg = [sb(f"xg{b}", [P, J, D]) for b in range(2)]
        mix = sb("mix", [P, 9600])
        parts = mix[0:NT, :].bitcast(BF16).rearrange("p (s t d) -> p s t d", s=3, t=HN)
        lo_all = mix[:, 0:KPAD]
        kk_all = mix[:, KPAD:2 * KPAD]
        bq_all = mix[:, 2 * KPAD:3 * KPAD]
        at = 3 * KPAD
        eaT = [mix[:, at + h * 512:at + h * 512 + 512].rearrange("p (j e) -> p j e", j=JH) for h in range(H)]
        at += 1024
        pre = [mix[:, at + h * 512:at + h * 512 + 512].rearrange("p (j e) -> p j e", j=JH) for h in range(H)]
        at += 1024
        msg = [mix[:, at + h * 512:at + h * 512 + 512].rearrange("p (j e) -> p j e", j=JH) for h in range(H)]
        assert at + 1024 <= 9600
        big = sb("big", [P, 12800])
        drow = big[:, 0:KPAD]
        srow = big[:, KPAD:2 * KPAD]
        drow_i, srow_i = drow.bitcast(I32), srow.bitcast(I32)
        drow_f = big[:, 2 * KPAD:3 * KPAD]
        srow_f = big[:, 3 * KPAD:4 * KPAD]
        iota8 = big[:, 4 * KPAD:4 * KPAD + NQ]
        below = big[:, 4 * KPAD + NQ:4 * KPAD + NQ + KC * NQ // 2].bitcast(BF16).rearrange("p (c q) -> p c q", c=KC)
        assert 4 * KPAD + NQ + KC * NQ // 2 <= 12800
        piece = [big[:, k * 1600:(k + 1) * 1600].bitcast(F16).rearrange("p (g t n) -> p g t n", g=DG, t=HP)
                 for k in range(NP_)]
        whot = big[:, 0:J * WW].rearrange("p (j w) -> p j w", j=J)
        ones_col = sb("ones_col", [P, 1], BF16)
        starts = sb("starts", [1, NQ], I32)
        starts_f = sb("starts_f", [1, NQ])
        tab = sb("tab", [P, CB], F16)
        tab0 = sb("tab0", [P, P], F16)
        key = [sb(f"key{n}", [P, 2, QT]) for n in range(2)]
        found = sb("found", [P, QT])
        fcol = sb("fcol", [P, 2])
        rel = sb("rel", [P, J])
        relm = sb("relm", [P, 2, J])
        hot = sb("hot", [P, J, W])
        vmax = sb("vmax", [P, J])
        vmin = sb("vmin", [P, J])
        viol = sb("viol", [P, 4])
        flag_f = sb("flag_f", [1, 2])
        flag = sb("flag", [1, 1], I32)
        dstf = sb("dstf", [P, 2, J])
        xc = [sb(f"xc{b}", [NT, TC, D]) for b in range(2)]
        st = sb("st", [NT, 12, TC])
        oc = [sb(f"oc{b}", [NT, TC, D]) for b in range(2)]

        psT2 = ps("psT", [P, J, P])
        psM2 = ps("psM", [P, J, D])
        psT = [psT2[:, h * JH:(h + 1) * JH, :] for h in range(H)]
        psM = [psM2[:, h * JH:(h + 1) * JH, :] for h in range(H)]
        psA = [ps(f"psA{b}", [P, WW]) for b in range(2)]
        psC2 = ps("psC", [P, 8, D])
        psN = psC2
        psC = [psC2[:, 4 * n:4 * n + 4, :].rearrange("p a b -> p (a b)")[:, 0:CB] for n in range(2)]
        psS = [psM2[0:1, 4 * n:4 * n + 4, :].rearrange("p a b -> p (a b)")[:, 0:NQ // 2] for n in range(2)]

        s_const = sem("s_const")
        s_ioc = sem("s_ioc")
        s_prep = sem("s_prep")
        s_wT = sem("s_wT")
        s_be = sem("s_be")
        s_bn = sem("s_bn")
        s_ready = sem("s_ready")
        s_ea = [sem(f"s_ea{b}") for b in range(2)]
        s_ix = [sem(f"s_ix{b}") for b in range(2)]
        s_xg = [sem(f"s_xg{b}") for b in range(2)]
        s_tr = [sem(f"s_tr{b}") for b in range(2)]
        s_eaT = sem("s_eaT")
        s_mm = sem("s_mm")
        s_pre = [sem(f"s_pre{b}") for b in range(2)]
        s_msg = sem("s_msg")
        s_ld = sem("s_ld")
        s_rel = sem("s_rel")
        s_hot = sem("s_hot")
        s_seg = sem("s_seg")
        s_acc = sem("s_acc")
        s_chk = sem("s_chk")
        s_chkp = sem("s_chkp")
        s_flag = sem("s_flag")
        g_in = [sem(f"g_in{l}") for l in range(2)]
        g_xg = [sem(f"g_xg{l}") for l in range(2)]
        g_tr = sem("g_tr")
        g_eaT = sem("g_eaT")
        g_mm = sem("g_mm")
        g_pre = sem("g_pre")
        g_msg = sem("g_msg")
        g_z = [sem(f"g_z{l}") for l in range(2)]
        g_df = [sem(f"g_df{l}") for l in range(2)]
        g_hot = [sem(f"g_hot{l}") for l in range(2)]
        g_seg = [sem(f"g_seg{l}") for l in range(2)]
        g_acc = [sem(f"g_acc{l}") for l in range(2)]
        e_clr = sem("e_clr")
        e_row = sem("e_row")
        e_f = sem("e_f")
        e_tr = sem("e_tr")
        e_cp = sem("e_cp")
        e_nm = sem("e_nm")
        e_bl = sem("e_bl")
        e_cnt = sem("e_cnt")
        e_st = sem("e_st")
        c_key = sem("c_key")
        c_hot = sem("c_hot")
        c_mm = sem("c_mm")
        c_ev = sem("c_ev")
        c_st = [sem(f"c_st{b}") for b in range(2)]
        p_sp = sem("p_sp")
        p_ld = [sem(f"p_ld{k}") for k in range(NP_)]
        p_us = sem("p_us")
        p_ev = sem("p_ev")
        flag2 = sb("flag2", [1, 1], I32)
        s_flag2 = sem("s_flag2")
        n_x = [[sem(f"n_x{l}{b}") for b in range(2)] for l in range(2)]
        n_xT = [sem(f"n_xT{l}") for l in range(2)]
        n_hT = [sem(f"n_hT{l}") for l in range(2)]
        n_h1 = sem("n_h1")
        n_a1 = sem("n_a1")
        n_h2 = [sem(f"n_h2{l}") for l in range(2)]
        n_ch = [sem(f"n_ch{l}") for l in range(2)]
        n_sq = [sem(f"n_sq{l}") for l in range(2)]
        n_aT = sem("n_aT")
        n_out = [[sem(f"n_out{l}{b}") for b in range(2)] for l in range(2)]
        s_through = sem("s_through")
        s_acc0 = sem("s_acc0")
        s_mask = sem("s_mask")
        g_mask = [sem(f"g_mask{l}") for l in range(2)]
        s_done = [sem(f"s_done{l}") for l in range(2)]

        psT_node = psT2[:, 0:TC, 0:NT]
        psN_node = psN[:, 0:TC, 0:NT]
        psM_node = psM2[0:NT, 0:TC, :]

        block = ctx.enter_context(nc.Block())

        def later(value):
            return not isinstance(value, int) or value > 0

        def edges(t, off):
            return t[bass.ds(off, GE)].rearrange("(p j) -> p j", j=J)

        def attrs(off):
            return ea[bass.ds(off, GE), :].rearrange("(p j) d -> p (j d)", j=J)

        def group_offset(i, b, last):
            return E - GE if last and b == 1 else i * (2 * GE) + b * GE

        def node_rows(t, c):
            return t[bass.ds(c * CN, CN), :].rearrange("(t p) d -> p t d", p=NT)

        SMALL = 3 + 2 + 6 + 3 + 1

        @block.sync
        def _(sp):
            sp.wait_ge(e_clr, 2)
            cut = KFULL * P * P
            for rows_i, t in ((drow_i, dst), (srow_i, src)):
                sp.dma_start(rows_i[:, 0:KFULL * P].rearrange("p (c e) -> p c e", c=KFULL),
                             t[0:cut].rearrange("(c p e) -> p c e", p=P, e=P)).then_inc(e_row, 16)
                sp.dma_start(rows_i[0:KT - KFULL * P, KFULL * P:KPAD],
                             t[cut:KT * P].rearrange("(p e) -> p e", e=P)).then_inc(e_row, 16)
                sp.dma_start(rows_i[KT - KFULL * P:KT - KFULL * P + 1, KFULL * P:KFULL * P + KREM],
                             t[KT * P:E].rearrange("(o e) -> o e", o=1)).then_inc(e_row, 16)
            for k, w in enumerate((We, W1, W2)):
                sp.dma_start(wrow[:, k, :], w).then_inc(s_const, 16)
            sp.dma_start(Wm_sb[:, :], Wm).then_inc(s_const, 16)
            sp.dma_start(Ws_sb[:, :], Wself).then_inc(s_const, 16)
            for k, v in enumerate((b1, bn_g, bn_b, bn_rm, bn_rv)):
                sp.dma_start(cols[:, k:k + 1], v.rearrange("(p o) -> p o", o=1)).then_inc(s_const, 16)
            sp.dma_start(cols[:, 5:6], eps.rearrange("(a o) -> a o", o=1).broadcast_to([P, 1])).then_inc(s_const, 16)
            for k, v in enumerate((b2, ln_g, ln_b)):
                sp.dma_start(rows[:, k, :], v.rearrange("(o d) -> o d", o=1).broadcast_to([P, D])).then_inc(s_const, 16)
            sp.dma_start(be_row[:, 0, :], be.rearrange("(o d) -> o d", o=1)).then_inc(s_const, 16)
            sp.wait_ge(s_prep, 5)
            for k in range(3):
                sp.dma_start(be3[k:k + 1, :], be_part[0:1, k, :]).then_inc(s_be, 16)

            def load(i, b, last):
                off = group_offset(i, b, last)
                if later(16 * J * i):
                    sp.wait_ge(s_xg[b], 16 * J * i)
                sp.sem_inc(s_through, 1)
                if later(2 * i + b - 1):
                    sp.wait_ge(s_acc, 2 * i + b - 1)
                sp.dma_start(srci[b][:, :], edges(src, off)).then_inc(s_ix[b], 16)
                sp.dma_start(dsti[b][:, :], edges(dst, off)).then_inc(s_ea[b], 16)
                if later(H * i):
                    sp.wait_ge(s_tr[b], H * i)
                sp.dma_start(ea_sb[b][:, :, :].rearrange("p j d -> p (j d)"), attrs(off)).then_inc(s_ea[b], 16)

            for b in range(2):
                load(0, b, False)
            with sp.Fori(1, PAIRS - 1) as i:
                for b in range(2):
                    load(i, b, False)
            for b in range(2):
                load(PAIRS - 1, b, True)

            def general_loads(l, sp_off, g):
                if later(g * NW):
                    sp.wait_ge(g_acc[l], g * NW)
                sp.dma_start(srci[0][:, :], edges(src, sp_off)).then_inc(g_in[l], 16)
                sp.dma_start(dsti[0][:, :], edges(dst, sp_off)).then_inc(g_in[l], 16)
                if l == 0:
                    sp.dma_start(ea_sb[0][:, :, :].rearrange("p j d -> p (j d)"), attrs(sp_off)).then_inc(g_in[l], 16)

            def general(l):
                sp.wait_ge((s_flag, s_flag2)[l], 1)
                v = sp.value_load((flag, flag2)[l][0:1, 0:1], min_val=0, max_val=1)
                with sp.If(v == 1):
                    general_loads(l, 0, 0)
                    with sp.Fori(1, G - 1) as g:
                        general_loads(l, g * GE, g)
                    general_loads(l, E - GE, G - 1)

            general(0)

            def nodes(l, source, target):
                sp.wait_ge(s_done[l], 1)
                def step(i):
                    for b in range(2):
                        c = i * 2 + b
                        if later(16 * i):
                            sp.wait_ge(n_out[l][b], 16 * i)
                        sp.dma_start(xc[b][:, :, :], node_rows(source, c)).then_inc(n_x[l][b], 16)
                    for b in range(2):
                        c = i * 2 + b
                        sp.wait_ge(n_ch[l], c * CH[l] + CH[l])
                        sp.dma_start(node_rows(target, c), oc[b][:, :, :]).then_inc(n_out[l][b], 16)

                step(0)
                with sp.Fori(1, CPAIRS) as i:
                    step(i)

                for b in range(2):
                    sp.wait_ge(n_out[l][b], 16 * CPAIRS)

            nodes(0, x, x2_dram)

            for b in range(2):
                sp.wait_ge(c_st[b], 16 * PAIRS)

            def dense_loads(c):
                for h in range(2):
                    for k in range(NP_):
                        if later(c * (2 * NP_) + (h * NP_ + k - NP_ + 1)):
                            sp.wait_ge(p_us, c * (2 * NP_) + (h * NP_ + k - NP_ + 1))
                        sp.dma_start(piece[k][:, :, :, :],
                                     counts[bass.ds(c * (2 * DG) + h * DG, DG), :, k * HP * GW:(k + 1) * HP * GW]
                                     .rearrange("g p (t n) -> p g t n", t=HP)).then_inc(p_ld[k], 16)

            dense_loads(0)
            with sp.Fori(1, DC) as c:
                dense_loads(c)
            sp.wait_ge(p_ev, 2 * DC)
            general(1)
            nodes(1, x2_dram, out)

        @block.gpsimd
        def _(pool):
            pool.memset(ident[:, :], 0.0).then_inc(s_ioc, 1)
            pool.memset(keep[:, :], 1.0).then_inc(s_ioc, 1)
            pool.memset(ones3[:, :], 1.0).then_inc(s_ioc, 1)
            pool.memset(ones_col[:, :], 1.0).then_inc(s_ioc, 1)
            pool.wait_ge(s_ioc, 4)
            pool.affine_select(out=ident[:, :], in_=ident[:, :], compare_op=ALU.not_equal, fill=1.0, base=0,
                               pattern=[[-1, P]], channel_multiplier=1).then_inc(s_ioc, 1)
            pool.affine_select(out=keep[:, :], in_=keep[:, :], compare_op=ALU.is_ge, fill=0.0, base=-DUP,
                               pattern=[[1, J]], channel_multiplier=J).then_inc(s_ioc, 1)
            pool.iota(iota[:, :], [[1, NPAD]], base=0, channel_multiplier=0,
                      allow_small_or_imprecise_dtypes=True).then_inc(s_ioc, 1)
            pool.iota(iota8, [[QN, NQ]], base=0, channel_multiplier=0,
                      allow_small_or_imprecise_dtypes=True).then_inc(s_ioc, 1)
            pool.iota(tab[:, :], [[1, CB]], base=1, channel_multiplier=0,
                      allow_small_or_imprecise_dtypes=True).then_inc(s_ioc, 1)
            pool.iota(tab0[:, :], [[1, P]], base=0, channel_multiplier=0,
                      allow_small_or_imprecise_dtypes=True).then_inc(s_ioc, 1)

            def gather(table, idx, rows_, signal):
                pool.sem_inc(s_through, 1)
                for j in range(J):
                    pool.indirect_dma_start(rows_[:, j, :], None, table,
                                            bass.IndirectOffsetOnAxis(ap=idx[:, j:j + 1], axis=0)).then_inc(signal, 16)

            def group(i, b):
                pool.wait_ge(s_ix[b], 16 * i + 16)
                if later(H * i):
                    pool.wait_ge(s_pre[b], H * i)
                gather(x[:, :], srci[b], xg[b], s_xg[b])

            for b in range(2):
                group(0, b)
            with pool.Fori(1, PAIRS) as i:
                for b in range(2):
                    group(i, b)

            def general(l, table):
                pool.wait_ge((s_flag, s_flag2)[l], 1)
                v = pool.value_load((flag, flag2)[l][0:1, 0:1], min_val=0, max_val=1)
                with pool.If(v == 1):
                    def group(g):
                        pool.wait_ge(g_in[l], g * (48 - 16 * l) + (48 - 16 * l))
                        if later(g * NW):
                            pool.wait_ge(g_acc[l], g * NW)
                        gather(table, srci[0], xg[0], g_xg[l])

                    group(0)
                    with pool.Fori(1, G) as g:
                        group(g)

            general(0, x[:, :])
            def split(i):
                for b in range(2):
                    c = i * 2 + b
                    pool.wait_ge(n_ch[0], c * CH[0] + CH[0])
                    part = [parts[:, k, bass.ds(c * TC, TC), :] for k in range(3)]
                    pool.tensor_copy(part[0], oc[b][:, :, :]).then_inc(p_sp, 1)
                    pool.wait_ge(p_sp, c * 5 + 1)
                    pool.sem_inc(s_through, 1)
                    pool.tensor_sub(rest[:, 0, :, :], oc[b][:, :, :], part[0]).then_inc(p_sp, 1)
                    pool.wait_ge(p_sp, c * 5 + 2)
                    pool.tensor_copy(part[1], rest[:, 0, :, :]).then_inc(p_sp, 1)
                    pool.wait_ge(p_sp, c * 5 + 3)
                    pool.sem_inc(s_through, 1)
                    pool.tensor_sub(rest[:, 1, :, :], rest[:, 0, :, :], part[1]).then_inc(p_sp, 1)
                    pool.wait_ge(p_sp, c * 5 + 4)
                    pool.tensor_copy(part[2], rest[:, 1, :, :]).then_inc(p_sp, 1)

            split(0)
            with pool.Fori(1, CPAIRS) as i:
                split(i)
            for b in range(2):
                pool.wait_ge(n_out[0][b], 16 * CPAIRS)
            general(1, x2_dram[:, :])

        @block.scalar
        def _(act):
            act.wait_ge(s_prep, 7)
            nc.scalar.activation(bn_t[:, 1:2], bn_t[:, 0:1], ACT.Sqrt).then_inc(s_bn, 1)
            for n_, (out_, ps_) in enumerate(((srow[:, 0:J * P], psT2[:, :, :]),
                                              (srow[:, J * P:KPAD], psC2[:, 0:KC - J, :]),
                                              (drow[:, 0:J * P], psM2[:, :, :]),
                                              (drow[:, J * P:KPAD], psT2[:, 0:KC - J, :]))):
                act.wait_ge(e_tr, n_ + 1)
                nc.scalar.copy(out_.rearrange("p (c e) -> p c e", e=P), ps_).then_inc(e_cp, 1)

            def group(i, b):
                g = i * 2 + b
                for h in range(H):
                    act.wait_ge(s_tr[b], H * i + h + 1)
                    if later(4 * i + 2 * b):
                        act.wait_ge(s_mm, 4 * i + 2 * b)
                    nc.scalar.copy(eaT[h][:, :, :], psT[h][:, :, :]).then_inc(s_eaT, 1)
                if later(16 * i):
                    act.wait_ge(c_st[b], 16 * i)
                for q in range(QG):
                    act.wait_ge(c_mm, g * QG + (q + 1))
                    nc.scalar.copy(cbuf[b][:, :, q * QN:(q + 1) * QN],
                                   psC[q % 2].rearrange("p (t n) -> p t n", t=HN)).then_inc(c_ev, 1)
                for h in range(H):
                    act.wait_ge(s_pre[b], H * i + h + 1)
                    if later(2 * i + b):
                        act.wait_ge(s_seg, 2 * i + b)
                    nc.scalar.activation(msg[h][:, :, :], pre[h][:, :, :], ACT.Relu).then_inc(s_msg, 1)
                act.wait_ge(c_ev, g * QG + QG)
                act.dma_start(counts[bass.ds(g, 1), :, :].rearrange("g p f -> (g p) f"),
                              cbuf[b][:, :, :].rearrange("p t n -> p (t n)")).then_inc(c_st[b], 16)

            for b in range(2):
                group(0, b)
            with act.Fori(1, PAIRS) as i:
                for b in range(2):
                    group(i, b)

            act.wait_ge(s_flag, 1)
            v = act.value_load(flag[0:1, 0:1], min_val=0, max_val=1)
            with act.If(v == 1):
                def general_group(g):
                    for h in range(H):
                        act.wait_ge(g_tr, g * H + (h + 1))
                        if later(g * H):
                            act.wait_ge(g_mm, g * H)
                        nc.scalar.copy(eaT[h][:, :, :], psT[h][:, :, :]).then_inc(g_eaT, 1)
                    for h in range(H):
                        act.wait_ge(g_pre, g * H + (h + 1))
                        if later(g * NW):
                            act.wait_ge(g_seg[0], g * NW)
                        nc.scalar.activation(msg[h][:, :, :], pre[h][:, :, :], ACT.Relu).then_inc(g_msg, 1)

                general_group(0)
                with act.Fori(1, G) as g:
                    general_group(g)

            def step(c):
                act.wait_ge(n_h1, c + 1)
                if later(c):
                    act.wait_ge(n_h2[0], c)
                nc.scalar.activation(aT[:, :, :], psT_node, ACT.Relu, bias=bn_bias[:, :],
                                     scale=bn_scale[:, :]).then_inc(n_a1, 1)
                for k in range(2):
                    act.wait_ge(n_ch[0], c * CH[0] + SQ[0][k])
                    nc.scalar.activation(z[:, 1, :, :], z[:, 0, :, :], ACT.Square).then_inc(n_sq[0], 1)
                    act.wait_ge(n_ch[0], c * CH[0] + RT[0][k])
                    nc.scalar.activation(st[:, 4, :], st[:, 3, :], ACT.Sqrt).then_inc(n_sq[0], 1)

            step(0)
            with act.Fori(1, 2 * CPAIRS) as c:
                step(c)

            def dense(c):
                for h in range(2):
                    act.wait_ge(p_us, c * (2 * NP_) + NP_ * (h + 1))
                    nc.scalar.copy(acc[:, bass.ds(c * (2 * DG * GW) + h * DG * GW, DG * GW)],
                                   psA[h][:, 0:DG * GW]).then_inc(p_ev, 1)

            dense(0)
            with act.Fori(1, DC) as c:
                dense(c)
            def step(c):
                act.wait_ge(n_xT[1], c + 1)
                if later(c):
                    act.wait_ge(n_h2[1], c)
                nc.scalar.copy(aT[:, :, :], psN_node).then_inc(n_aT, 1)
                act.wait_ge(n_ch[1], c * CH[1] + SQ[1][0])
                nc.scalar.activation(z[:, 1, :, :], z[:, 0, :, :], ACT.Square).then_inc(n_sq[1], 1)
                act.wait_ge(n_ch[1], c * CH[1] + RT[1][0])
                nc.scalar.activation(st[:, 4, :], st[:, 3, :], ACT.Sqrt).then_inc(n_sq[1], 1)

            step(0)
            with act.Fori(1, 2 * CPAIRS) as c:
                step(c)

        @block.vector
        def _(dve):
            nc.vector.memset(drow_i, -1).then_inc(e_clr, 1)
            nc.vector.memset(srow_i, -1).then_inc(e_clr, 1)
            nc.vector.memset(acc[:, :], 0.0).then_inc(s_acc0, 1)
            nc.vector.memset(found[:, :], 0.0).then_inc(s_acc0, 1)
            nc.vector.memset(vmax[:, :], 0.0).then_inc(s_acc0, 1)
            nc.vector.memset(vmin[:, :], 0.0).then_inc(s_acc0, 1)
            dve.wait_ge(s_const, 16 * SMALL)
            n = [0]

            def prep(ins):
                n[0] += 1
                ins.then_inc(s_prep, 1)
                dve.wait_ge(s_prep, n[0])

            prep(nc.vector.tensor_copy(be_part[:, 0, :], be_row[:, 0, :]))
            prep(nc.vector.tensor_sub(be_row[:, 1, :], be_row[:, 0, :], be_part[:, 0, :]))
            prep(nc.vector.tensor_copy(be_part[:, 1, :], be_row[:, 1, :]))
            prep(nc.vector.tensor_sub(be_row[:, 2, :], be_row[:, 1, :], be_part[:, 1, :]))
            prep(nc.vector.tensor_copy(be_part[:, 2, :], be_row[:, 2, :]))
            prep(nc.vector.tensor_scalar(one_eps[:, :], cols[:, 5:6], 1.0, None, ALU.add))
            prep(nc.vector.tensor_scalar(bn_t[:, 0:1], cols[:, 4:5], EPS, None, ALU.add))
            dve.wait_ge(s_bn, 1)
            prep(nc.vector.reciprocal(bn_t[:, 2:3], bn_t[:, 1:2]))
            prep(nc.vector.tensor_mul(bn_scale[:, :], bn_t[:, 2:3], cols[:, 1:2]))
            prep(nc.vector.tensor_sub(bn_t[:, 3:4], cols[:, 0:1], cols[:, 3:4]))
            prep(nc.vector.scalar_tensor_tensor(out=bn_bias[:, :], in0=bn_t[:, 3:4], scalar=bn_scale[:, :],
                                                in1=cols[:, 2:3], op0=ALU.mult, op1=ALU.add))
            dve.wait_ge(s_ioc, 10)
            prep(nc.vector.tensor_scalar(keep1[:, :], keep[:, :], -1.0, None, ALU.add))
            dve.wait_ge(s_wT, 1)
            for k, t in enumerate((WeT, W1T, W2T)):
                nc.vector.tensor_copy(t[:, :], psT[0][:, k, :]).then_inc(s_ready, 1)
            dve.wait_ge(s_acc0, 4)

            dve.wait_ge(e_row, 96)
            nc.vector.tensor_copy(srow_f, srow_i).then_inc(e_f, 1)
            nc.vector.tensor_copy(drow_f, drow_i).then_inc(e_f, 1)
            dve.wait_ge(e_f, 2)
            dve.wait_ge(s_ioc, 10)
            for c in range(KC):
                nc.vector.tensor_scalar(below[:, c, :], iota8, drow_f[:, c * P:c * P + 1], None,
                                        ALU.is_gt).then_inc(e_bl, 1)
            m = [0]

            def number(ins):
                m[0] += 1
                ins.then_inc(e_nm, 1)
                dve.wait_ge(e_nm, m[0])

            dve.wait_ge(e_cp, 2)
            number(nc.vector.tensor_scalar(lo_all, srow, 1.0 / NT, 0.5 / NT - 0.5, ALU.mult, ALU.add))
            number(nc.vector.tensor_scalar(kk_all, lo_all, ROUND, None, ALU.add))
            number(nc.vector.tensor_scalar(kk_all, kk_all, -ROUND, None, ALU.add))
            number(nc.vector.scalar_tensor_tensor(out=lo_all, in0=kk_all, scalar=-float(NT), in1=srow,
                                                  op0=ALU.mult, op1=ALU.add))
            dve.wait_ge(e_cp, 4)
            number(nc.vector.tensor_scalar(srow, drow, 1.0 / QN, 0.5 / QN - 0.5, ALU.mult, ALU.add))
            number(nc.vector.tensor_scalar(srow, srow, ROUND, None, ALU.add))
            number(nc.vector.tensor_scalar(bq_all, srow, -ROUND, None, ALU.add))
            number(nc.vector.scalar_tensor_tensor(out=drow, in0=bq_all, scalar=-float(QN), in1=drow,
                                                  op0=ALU.mult, op1=ALU.add))
            number(nc.vector.scalar_tensor_tensor(out=kk_all, in0=kk_all, scalar=float(QN), in1=drow,
                                                  op0=ALU.mult, op1=ALU.add))
            number(nc.vector.tensor_scalar(kk_all, kk_all, 1.0, None, ALU.add))
            dve.wait_ge(e_cnt, 1)
            for n_ in range(2):
                nc.vector.tensor_scalar(starts_f[:, n_ * (NQ // 2):(n_ + 1) * (NQ // 2)], psS[n_],
                                        -float(KPAD - KT), 0.0, ALU.add, ALU.max).then_inc(e_st, 1)
            dve.wait_ge(e_st, 2)
            nc.vector.tensor_scalar(starts[:, :], starts_f[:, :], float(KT + 1 - QT), None,
                                    ALU.min).then_inc(e_st, 1)
            dve.wait_ge(e_st, 3)

            def block(g, q):
                n_ = q % 2
                dve.sem_inc(s_through, 1)
                first = dve.value_load(starts[0:1, bass.ds(g * QG + q, 1)], min_val=0, max_val=KT + 1 - QT)
                if later(g * QG + (q - 1)):
                    dve.wait_ge(c_mm, g * QG + (q - 1))
                    dve.wait_ge(c_hot, g * QG + (q - 1))
                nc.vector.tensor_copy(key[n_][:, 0, :], lo_all[:, bass.ds(first, QT)]).then_inc(c_key, 1)
                nc.vector.scalar_tensor_tensor(out=key[n_][:, 1, :], in0=bq_all[:, bass.ds(first, QT)],
                                               scalar=iota[:, bass.ds(g * QG + q, 1)],
                                               in1=kk_all[:, bass.ds(first, QT)],
                                               op0=ALU.is_equal, op1=ALU.mult).then_inc(c_key, 1)
                dve.wait_ge(c_key, g * (3 * QG) + (3 * q + 2))
                nc.vector.scalar_tensor_tensor(out=found[:, :], in0=key[n_][:, 1, :], scalar=1.0, in1=found[:, :],
                                               op0=ALU.min, op1=ALU.add).then_inc(c_key, 1)
                for t in range(QT):
                    nc.vector.tensor_scalar(Lh[n_][:, t, :], tab0[:, :], key[n_][:, 0, t:t + 1], None, ALU.is_equal)
                    ins = nc.vector.tensor_scalar(Rh[n_][:, t, :], tab[:, :], key[n_][:, 1, t:t + 1], None,
                                                  ALU.is_equal)
                ins.then_inc(c_hot, 1)
                dve.wait_ge(c_key, g * (3 * QG) + (3 * q + 3))

            hot_in1 = iota[:, 0:W].unsqueeze(1).broadcast_to([P, J, W])

            def base_of(idx):
                dve.sem_inc(s_through, 1)
                return dve.value_load(idx[0:1, 0:1], min_val=0, max_val=N - 1)

            def masked(where, signal):
                nc.vector.tensor_mul(relm[:, 0, :], where, keep[:, :]).then_inc(signal, 1)
                dve.wait_ge(signal, 1)
                nc.vector.tensor_add(relm[:, 1, :], relm[:, 0, :], keep1[:, :]).then_inc(signal, 1)
                dve.wait_ge(signal, 2)
                return relm[:, 1, :]

            def add(g, b):
                base = base_of(dsti[b])
                dve.wait_ge(s_seg, g + 1)
                if later(g):
                    dve.wait_ge(s_acc, g)
                nc.vector.tensor_add(acc[:, bass.ds(base, W)], acc[:, bass.ds(base, W)],
                                     psA[0][:, 0:W]).then_inc(s_acc, 1)

            def group(i, b, last):
                g = i * 2 + b
                dve.wait_ge(s_ea[b], 32 * i + 32)
                base = base_of(dsti[b])
                if later(g):
                    dve.wait_ge(s_hot, g)
                nc.vector.tensor_scalar(rel[:, :], dsti[b][:, :], iota[:, bass.ds(base, 1)], None,
                                        ALU.subtract).then_inc(s_rel, 1)
                dve.wait_ge(s_rel, g * 3 + 1)
                nc.vector.tensor_tensor(vmax[:, :], vmax[:, :], rel[:, :], ALU.max).then_inc(s_rel, 1)
                nc.vector.tensor_tensor(vmin[:, :], vmin[:, :], rel[:, :], ALU.min).then_inc(s_rel, 1)
                dve.wait_ge(s_rel, g * 3 + 3)
                for q in range(QG):
                    block(g, q)
                    if q == 1:
                        if later(g):
                            add(g - 1, 1 - b)
                        where = masked(rel[:, :], s_mask) if last and b == 1 else rel[:, :]
                        nc.vector.tensor_tensor(hot[:, :, :], where.unsqueeze(2).broadcast_to([P, J, W]), hot_in1,
                                                ALU.is_equal).then_inc(s_hot, 1)
                dve.wait_ge(s_xg[b], 16 * J * i + 16 * J)
                if later(2 * g):
                    dve.wait_ge(s_msg, 2 * g)
                for h in range(H):
                    dve.wait_ge(s_mm, g * 2 + (h + 1))
                    nc.vector.tensor_add(pre[h][:, :, :], psM[h][:, :, :],
                                         xg[b][:, h * JH:(h + 1) * JH, :]).then_inc(s_pre[b], 1)
            for b in range(2):
                group(0, b, False)
            with dve.Fori(1, PAIRS - 1) as i:
                for b in range(2):
                    group(i, b, False)
            for b in range(2):
                group(PAIRS - 1, b, True)

            add(G - 1, 1)

            k = [0]

            def chk(ins):
                k[0] += 1
                ins.then_inc(s_chk, 1)
                dve.wait_ge(s_chk, k[0])

            chk(nc.vector.tensor_reduce(viol[:, 0:1], vmax[:, :], axis=AX, op=ALU.max))
            chk(nc.vector.tensor_reduce(viol[:, 1:2], vmin[:, :], axis=AX, op=ALU.min))
            chk(nc.vector.tensor_scalar(viol[:, 2:3], viol[:, 0:1], float(-(W - 1)), None, ALU.add))
            chk(nc.vector.tensor_scalar(viol[:, 3:4], viol[:, 1:2], -1.0, None, ALU.mult))
            chk(nc.vector.tensor_max(viol[:, 0:1], viol[:, 2:3], viol[:, 3:4]))
            chk(nc.vector.tensor_reduce(fcol[:, 0:1], found[:, :], axis=AX, op=ALU.add))
            dve.wait_ge(s_chkp, 1)
            chk(nc.vector.tensor_reduce(flag_f[:, 1:2], psA[1][0:1, P:2 * P], axis=AX, op=ALU.add))
            nc.vector.tensor_scalar(flag2[:, :], flag_f[:, 1:2], float(E), None, ALU.not_equal).then_inc(s_flag2, 1)
            chk(nc.vector.tensor_reduce(flag_f[:, 0:1], psA[1][0:1, 0:P], axis=AX, op=ALU.max))
            nc.vector.tensor_scalar(flag[:, :], flag_f[:, 0:1], 0.0, None, ALU.is_gt).then_inc(s_flag, 1)

            def general_group(l, g, last):
                dve.wait_ge(g_in[l], g * (48 - 16 * l) + (48 - 16 * l))
                if later(g * NW):
                    dve.wait_ge(g_acc[l], g * NW)
                nc.vector.tensor_copy(dstf[:, 0, :], dsti[0][:, :]).then_inc(g_df[l], 1)
                dve.wait_ge(g_df[l], g + 1)
                where = masked(dstf[:, 0, :], g_mask[l]) if last else dstf[:, 0, :]
                if l == 0:
                    dve.wait_ge(g_xg[l], g * (16 * J) + 16 * J)
                    if later(g * H):
                        dve.wait_ge(g_msg, g * H)
                    for h in range(H):
                        dve.wait_ge(g_mm, g * H + (h + 1))
                        nc.vector.tensor_add(pre[h][:, :, :], psM[h][:, :, :],
                                             xg[0][:, h * JH:(h + 1) * JH, :]).then_inc(g_pre, 1)
                dve.sem_inc(s_through, 1)
                with dve.Fori(0, NW) as w:
                    nc.vector.tensor_tensor(whot[:, :, :], where.unsqueeze(2).broadcast_to([P, J, WW]),
                                            iota[:, bass.ds(w * WW, WW)].unsqueeze(1).broadcast_to([P, J, WW]),
                                            ALU.is_equal).then_inc(g_hot[l], 1)
                    dve.wait_ge(g_seg[l], g * NW + w + 1)
                    nc.vector.tensor_add(acc[:, bass.ds(w * WW, WW)], acc[:, bass.ds(w * WW, WW)],
                                         psA[0][:, :]).then_inc(g_acc[l], 1)
                    dve.wait_ge(g_acc[l], g * NW + w + 1)

            def general(l):
                dve.wait_ge((s_flag, s_flag2)[l], 1)
                v = dve.value_load((flag, flag2)[l][0:1, 0:1], min_val=0, max_val=1)
                with dve.If(v == 1):
                    nc.vector.memset(acc[:, :], 0.0).then_inc(g_z[l], 1)
                    dve.wait_ge(g_z[l], 1)
                    general_group(l, 0, False)
                    with dve.Fori(1, G - 1) as g:
                        general_group(l, g, False)
                    general_group(l, G - 1, True)
                    dve.wait_ge(g_acc[l], G * NW)

            dve.wait_ge(s_acc, G)
            general(0)
            nc.vector.memset(st[:, 11, :], 0.0).then_inc(s_done[0], 1)

            for b in range(2):
                dve.wait_ge(c_st[b], 16 * PAIRS)

            def chain(l, c):
                k = [0]

                def link(ins):
                    k[0] += 1
                    ins.then_inc(n_ch[l], 1)
                    dve.wait_ge(n_ch[l], c * CH[l] + k[0])
                    return k[0]
                return link

            def per_row(col):
                return st[:, col, :].unsqueeze(2).broadcast_to([NT, TC, D])

            def norm(l, c, link, slot, which, result):
                link(nc.vector.tensor_reduce(st[:, 0, :], z[:, slot, :, :], axis=AX, op=ALU.add))
                link(nc.vector.tensor_scalar(st[:, 1, :], st[:, 0, :], 1.0 / D, None, ALU.mult))
                at = link(nc.vector.tensor_sub(z[:, 0, :, :], z[:, slot, :, :], per_row(1)))
                assert at == SQ[l][which], at
                dve.wait_ge(n_sq[l], c * (2 * len(SQ[l])) + 2 * which + 1)
                link(nc.vector.tensor_reduce(st[:, 2, :], z[:, 1, :, :], axis=AX, op=ALU.add))
                at = link(nc.vector.tensor_scalar(st[:, 3, :], st[:, 2, :], 1.0 / D, EPS, ALU.mult, ALU.add))
                assert at == RT[l][which], at
                dve.wait_ge(n_sq[l], c * (2 * len(SQ[l])) + 2 * which + 2)
                link(nc.vector.reciprocal(st[:, 5, :], st[:, 4, :]))
                link(nc.vector.tensor_mul(result, z[:, 0, :, :], per_row(5)))

            def param(k):
                return rows[0:NT, k, :].unsqueeze(1).broadcast_to([NT, TC, D])

            def step(i):
                for b in range(2):
                    c = i * 2 + b
                    link = chain(0, c)
                    dve.wait_ge(n_xT[0], c + 1)
                    if later(c):
                        dve.wait_ge(n_h1, c)
                    nc.vector.scalar_tensor_tensor(
                        out=hT[:, :, :], in0=psN_node, scalar=one_eps[:, :],
                        in1=acc[:, bass.ds(c * CN, CN)].rearrange("d (t n) -> d t n", t=TC),
                        op0=ALU.mult, op1=ALU.add).then_inc(n_hT[0], 1)
                    dve.wait_ge(n_h2[0], c + 1)
                    if later(c * CH[0]):
                        dve.wait_ge(n_ch[0], c * CH[0])
                    link(nc.vector.tensor_add(z[:, 2, :, :], psM_node, param(0)))
                    norm(0, c, link, 2, 0, z[:, 3, :, :])
                    link(nc.vector.tensor_mul(z[:, 2, :, :], z[:, 3, :, :], param(1)))
                    link(nc.vector.tensor_add(z[:, 3, :, :], z[:, 2, :, :], param(2)))
                    link(nc.vector.tensor_add(z[:, 2, :, :], z[:, 3, :, :], xc[b][:, :, :]))
                    link(nc.vector.scalar_tensor_tensor(out=z[:, 3, :, :], in0=z[:, 2, :, :], scalar=0.0,
                                                        in1=xc[b][:, :, :], op0=ALU.max, op1=ALU.add))
                    if later(16 * i):
                        dve.wait_ge(n_out[0][b], 16 * i)
                        dve.wait_ge(p_sp, c * 5 - 5)
                    norm(0, c, link, 3, 1, oc[b][:, :, :])

            step(0)
            with dve.Fori(1, CPAIRS) as i:
                step(i)

            dve.wait_ge(p_ev, 2 * DC)
            general(1)
            nc.vector.memset(st[:, 11, :], 0.0).then_inc(s_done[1], 1)

            def step(i):
                for b in range(2):
                    c = i * 2 + b
                    link = chain(1, c)
                    if later(c):
                        dve.wait_ge(n_h2[1], c)
                    nc.vector.tensor_copy(hT[:, :, :], acc[:, bass.ds(c * CN, CN)].rearrange(
                        "d (t n) -> d t n", t=TC)).then_inc(n_hT[1], 1)
                    dve.wait_ge(n_h2[1], c + 1)
                    if later(c * CH[1]):
                        dve.wait_ge(n_ch[1], c * CH[1])
                    link(nc.vector.tensor_add(z[:, 2, :, :], psM_node, xc[b][:, :, :]))
                    if later(16 * i):
                        dve.wait_ge(n_out[1][b], 16 * i)
                    norm(1, c, link, 2, 0, oc[b][:, :, :])

            step(0)
            with dve.Fori(1, CPAIRS) as i:
                step(i)

        @block.tensor
        def _(pe):
            pe.wait_ge(s_const, 16 * SMALL)
            pe.wait_ge(s_ioc, 10)
            for k in range(3):
                last_ = nc.tensor.transpose(psT[0][:, k, :], wrow[:, k, :], ident[:, :])
            last_.then_inc(s_wT, 1)
            pe.wait_ge(s_ready, 3)
            pe.wait_ge(e_f, 2)
            for n_, (in_, c0, out_) in enumerate(((srow_f, 0, psT2), (srow_f, J, psC2),
                                                  (drow_f, 0, psM2), (drow_f, J, psT2))):
                if n_ == 3:
                    pe.wait_ge(e_cp, 1)
                for c in range(c0, min(c0 + J, KC)):
                    ins = nc.tensor.transpose(out_[:, c - c0, :], in_[:, c * P:(c + 1) * P], ident[:, :])
                ins.then_inc(e_tr, 1)
            pe.wait_ge(e_cp, 3)
            pe.wait_ge(e_bl, KC)
            for c in range(KC):
                for n_ in range(2):
                    ins = nc.tensor.matmul(psS[n_], ones_col[:, :], below[:, c, n_ * (NQ // 2):(n_ + 1) * (NQ // 2)],
                                           start=c == 0, stop=c == KC - 1)
            ins.then_inc(e_cnt, 1)
            pe.wait_ge(e_cp, 4)
            pe.wait_ge(e_st, 2)
            pe.wait_ge(s_be, 48)

            def block(g, q):
                pe.wait_ge(c_hot, g * QG + (q + 1))
                if later(g * QG + (q - 1)):
                    pe.wait_ge(c_ev, g * QG + (q - 1))
                for t in range(QT):
                    ins = nc.tensor.matmul(psC[q % 2], Lh[q % 2][:, t, :], Rh[q % 2][:, t, :], start=t == 0,
                                           stop=t == QT - 1)
                ins.then_inc(c_mm, 1)

            def transpose_group(b, signal):
                for h in range(H):
                    for j in range(JH):
                        ins = nc.tensor.transpose(psT[h][:, j, :], ea_sb[b][:, h * JH + j, :], ident[:, :])
                    ins.then_inc(signal, 1)

            def project(h, signal):
                nc.tensor.matmul(psM[h][:, :, :], ones3[:, :], be3[:, :].unsqueeze(1).broadcast_to([3, JH, D]),
                                 start=True, stop=False)
                for j in range(JH):
                    ins = nc.tensor.matmul(psM[h][:, j, :], eaT[h][:, j, :], WeT[:, :], start=False,
                                           stop=j == JH - 1)
                ins.then_inc(signal, 1)

            def group(i, b):
                g = i * 2 + b
                pe.wait_ge(s_ea[b], 32 * i + 32)
                if later(2 * g):
                    pe.wait_ge(s_eaT, 2 * g)
                transpose_group(b, s_tr[b])
                block(g, 0)
                if later(H * (i + b)):
                    pe.wait_ge(s_pre[1 - b], H * (i + b))
                for h in range(H):
                    pe.wait_ge(s_eaT, g * 2 + (h + 1))
                    project(h, s_mm)
                for q in range(1, QG):
                    block(g, q)
                pe.wait_ge(s_hot, g + 1)
                if later(g):
                    pe.wait_ge(s_acc, g)
                for h in range(H):
                    pe.wait_ge(s_msg, g * 2 + (h + 1))
                    for j in range(JH):
                        ins = nc.tensor.matmul(psA[0][:, 0:W], msg[h][:, j, :], hot[:, h * JH + j, :],
                                               start=h + j == 0, stop=h * JH + j == J - 1)
                ins.then_inc(s_seg, 1)

            for b in range(2):
                group(0, b)
            with pe.Fori(1, PAIRS) as i:
                for b in range(2):
                    group(i, b)

            pe.wait_ge(s_chk, 6)
            nc.tensor.matmul(psA[1][0:1, P:2 * P], fcol[:, 0:1], ident[:, :], start=True, stop=True)
            nc.tensor.matmul(psA[1][0:1, 0:P], viol[:, 0:1], ident[:, :], start=True, stop=True).then_inc(s_chkp, 1)

            def general(l):
                pe.wait_ge((s_flag, s_flag2)[l], 1)
                v = pe.value_load((flag, flag2)[l][0:1, 0:1], min_val=0, max_val=1)
                with pe.If(v == 1):
                    def group(g):
                        if l == 0:
                            pe.wait_ge(g_in[l], g * 48 + 48)
                            if later(g * H):
                                pe.wait_ge(g_eaT, g * H)
                            transpose_group(0, g_tr)
                            if later(g * H):
                                pe.wait_ge(g_pre, g * H)
                            for h in range(H):
                                pe.wait_ge(g_eaT, g * H + (h + 1))
                                project(h, g_mm)
                            pe.wait_ge(g_msg, g * H + H)
                        else:
                            pe.wait_ge(g_xg[l], g * (16 * J) + 16 * J)
                        pe.sem_inc(s_through, 1)
                        with pe.Fori(0, NW) as w:
                            pe.wait_ge(g_hot[l], g * NW + w + 1)
                            for j in range(J):
                                rows_ = msg[j // JH][:, j % JH, :] if l == 0 else xg[0][:, j, :]
                                ins = nc.tensor.matmul(psA[0][:, :], rows_, whot[:, j, :], start=j == 0,
                                                       stop=j == J - 1)
                            ins.then_inc(g_seg[l], 1)

                    group(0)
                    with pe.Fori(1, G) as g:
                        group(g)

            general(0)

            def step(i):
                for b in range(2):
                    c = i * 2 + b
                    pe.wait_ge(n_x[0][b], 16 * i + 16)
                    if later(c):
                        pe.wait_ge(n_hT[0], c)
                    for t in range(TC):
                        ins = nc.tensor.transpose(psN[:, t, 0:NT], xc[b][:, t, :], ident[0:NT, 0:NT])
                    ins.then_inc(n_xT[0], 1)
                    pe.wait_ge(n_hT[0], c + 1)
                    if later(c):
                        pe.wait_ge(n_a1, c)
                    for t in range(TC):
                        ins = nc.tensor.matmul(psT2[:, t, 0:NT], W1T[:, :], hT[:, t, :], start=True, stop=True)
                    ins.then_inc(n_h1, 1)
                    pe.wait_ge(n_a1, c + 1)
                    if later(c * CH[0]):
                        pe.wait_ge(n_ch[0], c * CH[0])
                    for t in range(TC):
                        ins = nc.tensor.matmul(psM2[0:NT, t, :], aT[:, t, :], W2T[:, :], start=True, stop=True)
                    ins.then_inc(n_h2[0], 1)

            step(0)
            with pe.Fori(1, CPAIRS) as i:
                step(i)

            def dense(c):
                for h in range(2):
                    if later(c * 2 + (h - 1)):
                        pe.wait_ge(p_ev, c * 2 + (h - 1))
                    for k in range(NP_):
                        pe.wait_ge(p_ld[k], c * 32 + 16 * (h + 1))
                        for t in range(HP):
                            for part in range(3):
                                ins = nc.tensor.matmul(
                                    psA[h][:, 0:DG * GW].rearrange("p (g n) -> p g n", g=DG),
                                    parts[:, part, k * HP + t, :], piece[k][0:NT, :, t, :],
                                    start=k + t + part == 0, stop=k * HP + t == HN - 1 and part == 2)
                        ins.then_inc(p_us, 1)

            pe.wait_ge(p_sp, 5 * DC)
            dense(0)
            with pe.Fori(1, DC) as c:
                dense(c)
            general(1)

            def step(i):
                for b in range(2):
                    c = i * 2 + b
                    pe.wait_ge(n_x[1][b], 16 * i + 16)
                    if later(c):
                        pe.wait_ge(n_aT, c)
                    for t in range(TC):
                        ins = nc.tensor.transpose(psN[:, t, 0:NT], xc[b][:, t, :], ident[0:NT, 0:NT])
                    ins.then_inc(n_xT[1], 1)
                    pe.wait_ge(n_hT[1], c + 1)
                    pe.wait_ge(n_aT, c + 1)
                    if later(c * CH[1]):
                        pe.wait_ge(n_ch[1], c * CH[1])
                    for t in range(TC):
                        nc.tensor.matmul(psM2[0:NT, t, :], hT[:, t, :], Wm_sb[:, :], start=True, stop=False)
                        ins = nc.tensor.matmul(psM2[0:NT, t, :], aT[:, t, :], Ws_sb[:, :], start=False, stop=True)
                    ins.then_inc(n_h2[1], 1)

            step(0)
            with pe.Fori(1, CPAIRS) as i:
                step(i)

_INS = ["x", "src", "dst", "edge_attr_128", "L0_gnn_eps", "L0_gnn_We", "L0_gnn_be", "L0_gnn_W1", "L0_gnn_b1",
        "L0_gnn_bn_g", "L0_gnn_bn_b", "L0_gnn_bn_rm", "L0_gnn_bn_rv", "L0_gnn_W2", "L0_gnn_b2", "L0_gnn_ln_g",
        "L0_gnn_ln_b", "L1_gnn_W", "L1_gnn_W_self"]


def kernel(**inputs):
    import concourse.bacc as bacc
    from concourse.bass_utils import run_bass_kernel_spmd

    nc = bacc.Bacc("TRN2", target_bir_lowering=False, num_devices=1)
    arrays, args = {}, []
    for name in _INS:
        a = np.ascontiguousarray(inputs[name])
        if a.ndim == 0:
            a = a.reshape(1)
        arrays[f"in_{name}"] = a
        args.append(nc.dram_tensor(f"in_{name}", a.shape, mybir.dt.from_np(a.dtype), kind="ExternalInput").ap())
    n = inputs["x"].shape[0]
    out = nc.dram_tensor("out_rows", (n, D), F32, kind="ExternalOutput").ap()
    program(nc, *args, out)
    r = run_bass_kernel_spmd(nc, [arrays], core_ids=[0])
    return r.results[0]["out_rows"]
```

```python
import numpy as np
import concourse.bass as bass
from concourse import mybir

F32 = mybir.dt.float32
BF16 = mybir.dt.bfloat16
F16 = mybir.dt.float16
I32 = mybir.dt.int32
ALU = mybir.AluOpType
ACT = mybir.ActivationFunctionType
AX = mybir.AxisListType.X

P = 128
D = 128
J = 8
H = 2
JH = J // H
GE = P * J
W = 40
WW = 512
NT = 125
TC = 5
CN = NT * TC
QN = 8
QT = 3
SH = 4
QG = 4
HN = 50
CB = HN * QN
GW = QG * QN
DG = 10
HP = 10
NP_ = HN // HP
EARLY = 2
ROUND = 12582912.0
EPS = 1e-5
CA = 10
CO = 7
CH = 8


def program(nc, x, src, dst, ea, eps, We, be, W1, b1, bn_g, bn_b, bn_rm, bn_rv, W2, b2, ln_g, ln_b,
            Wm, Wself, out):
    N = x.shape[0]
    E = src.shape[0]
    G = -(-E // GE)
    PAIRS = G // 2
    assert G == 2 * PAIRS and N % (2 * CN) == 0
    DUP = G * GE - E
    CPAIRS = N // (2 * CN)
    NW = -(-N // WW)
    NPAD = NW * WW
    assert NPAD >= N + W
    KT = E // P
    KREM = E - KT * P
    KC = -(-(KT + 1) // P)
    KPAD = KC * P
    KFULL = KT // P
    NQ = QG * G
    PLANE = 3 * KPAD
    SE = P // SH
    UPAD = SH * KPAD - (-(-E // SE))
    UMAX = SH * (KT + 1 - QT) + SH - 1
    SLOTS = 11
    DC = 10
    assert HN * NT == N and DC * CN == N and DC * 2 * DG * GW >= N and NQ * QN >= N and KREM > 0

    x2_dram = nc.dram_tensor("x2_rows", (N, D), F32, kind="Internal").ap()
    xb_dram = nc.dram_tensor("x_plus_be", (N, D), F32, kind="Internal").ap()
    counts = nc.dram_tensor("counts", (G, P, HN * GW), F16, kind="Internal").ap()

    from contextlib import ExitStack
    ctx = ExitStack()
    with ctx:
        def sb(name, shape, dt=F32):
            return ctx.enter_context(nc.sbuf_tensor(name, shape, dt))

        def ps(name, shape):
            return ctx.enter_context(nc.psum_tensor(name, shape, F32))

        def sem(name):
            return ctx.enter_context(nc.semaphore(name))

        acc = sb("acc", [P, NPAD])
        iota = sb("iota", [P, NPAD])
        ident = sb("ident", [P, P])
        keep = sb("keep", [P, J])
        keep1 = sb("keep1", [P, J])
        wrow = sb("wrow", [P, 3, D])
        WeT = sb("WeT", [P, D])
        W1T = sb("W1T", [P, D])
        W2T = sb("W2T", [P, D])
        Wm_sb = sb("Wm_sb", [P, D])
        Ws_sb = sb("Ws_sb", [P, D])
        cols = sb("cols", [P, 8])
        bn_scale = sb("bn_scale", [P, 1])
        bn_bias = sb("bn_bias", [P, 1])
        bn_t = sb("bn_t", [P, 4])
        one_eps = sb("one_eps", [P, 1])
        rows = sb("rows", [P, 3, D])
        be_bc = sb("be_bc", [P, D])

        reg = sb("reg", [P, 6816])
        Rh = [reg[:, n * 600:(n + 1) * 600].bitcast(BF16).rearrange("p (t c) -> p t c", t=QT) for n in range(QG)]
        Lh = [reg[:, 2400 + n * 192:2592 + n * 192].bitcast(BF16).rearrange("p (c t) -> p c t", t=QT)
              for n in range(QG)]
        cbuf = [reg[:, 3168 + b * 800:3968 + b * 800].bitcast(F16).rearrange("p (t n) -> p t n", t=HN)
                for b in range(2)]
        assert Rh[0].shape[2] == CB and QT * CB // 2 <= 600 and QT * P // 2 <= 192
        ea_sb = [reg[:, 4768 + b * 1024:5792 + b * 1024].rearrange("p (j d) -> p j d", j=J) for b in range(2)]
        z = reg[0:NT, 0:8 * TC * D].rearrange("p (s t d) -> p s t d", s=8, t=TC)
        below = [reg[:, n * NQ // 2:(n + 1) * NQ // 2].bitcast(BF16) for n in range(SLOTS)]
        hT = reg[:, 5120:5745].rearrange("p (t n) -> p t n", t=TC)
        aT = reg[:, 5760:6385].rearrange("p (t n) -> p t n", t=TC)
        srci = [sb(f"srci{b}", [P, J], I32) for b in range(2)]
        dsti = [sb(f"dsti{b}", [P, J], I32) for b in range(2)]
        xg = [sb(f"xg{b}", [P, J, D]) for b in range(2)]
        rest = [t[0:NT, 0:TC, :] for t in xg]
        mix = sb("mix", [P, 9600])
        parts = mix[0:NT, :].bitcast(BF16).rearrange("p (s t d) -> p s t d", s=3, t=HN)
        lo_f = mix[:, 0:KPAD]
        kk_f = mix[:, KPAD:2 * KPAD]
        at = 3 * KPAD
        eaT = [mix[:, at + h * 512:at + h * 512 + 512].rearrange("p (j e) -> p j e", j=JH) for h in range(H)]
        at += 1024
        pre = [mix[:, at + h * 512:at + h * 512 + 512].rearrange("p (j e) -> p j e", j=JH) for h in range(H)]
        at += 1024
        msg = [mix[:, at + h * 512:at + h * 512 + 512].rearrange("p (j e) -> p j e", j=JH) for h in range(H)]
        assert at + 1024 <= 9600
        big = sb("big", [P, 12800])
        num = big[:, 0:SH * PLANE // 2].bitcast(F16)
        XR = N // P
        xh = [big[:, h * (XR // 2) * D:(h + 1) * (XR // 2) * D].rearrange("p (r d) -> p r d", d=D) for h in range(2)]
        xr = big[0:N - XR * P, XR * D:(XR + 1) * D]
        drow, srow, drow_f, srow_f = (acc[:, k * KPAD:(k + 1) * KPAD] for k in range(4))
        drow_i, srow_i = drow.bitcast(I32), srow.bitcast(I32)
        assert 4 * KPAD <= NPAD and SH * PLANE // 2 <= 12800
        piece = [big[:, k * 1600:(k + 1) * 1600].bitcast(F16).rearrange("p (g t n) -> p g t n", g=DG, t=HP)
                 for k in range(NP_)]
        whot = big[:, 0:J * WW].rearrange("p (j w) -> p j w", j=J)
        ones_col = sb("ones_col", [P, 1], BF16)
        iota16 = sb("iota16", [P, NQ], F16)
        fb = sb("fb", [P, KC * SH])
        starts = sb("starts", [1, NQ], I32)
        starts_f = mix[0:1, 2 * KPAD:2 * KPAD + NQ]
        starts_k = mix[0:1, 2 * KPAD + NQ:2 * KPAD + 2 * NQ]
        starts_s = lo_f[0:1, 0:NQ]
        bases = sb("bases", [1, G + 1], I32)
        tab = sb("tab", [P, CB], F16)
        tab0 = sb("tab0", [P, P, QT], F16)
        key = [sb(f"key{n}", [P, QG * QT]) for n in range(2)]
        found = sb("found", [P, QG * QT])
        fcol = sb("fcol", [P, 2])
        rel = sb("rel", [P, J])
        relm = sb("relm", [P, 2, J])
        hot = sb("hot", [P, J, W])
        vmax = sb("vmax", [P, J])
        vmin = sb("vmin", [P, J])
        viol = sb("viol", [P, 4])
        flag_f = sb("flag_f", [1, 2])
        flag = sb("flag", [1, 1], I32)
        flag2 = sb("flag2", [1, 1], I32)
        dstf = sb("dstf", [P, 2, J])
        xc = [sb(f"xc{b}", [NT, TC, D]) for b in range(2)]
        st = sb("st", [NT, 13, TC])
        oc = [sb(f"oc{b}", [NT, TC, D]) for b in range(2)]

        psT2 = ps("psT", [P, J, P])
        psM2 = ps("psM", [P, J, D])
        psT = [psT2[:, h * JH:(h + 1) * JH, :] for h in range(H)]
        psM = [psM2[:, h * JH:(h + 1) * JH, :] for h in range(H)]
        psA = [ps(f"psA{b}", [P, WW]) for b in range(2)]
        psC2 = ps("psC", [P, 8, D])
        psN = psC2
        psC = [psC2[:, 4 * n:4 * n + 4, :].rearrange("p a b -> p (a b)")[:, 0:CB] for n in range(2)]
        psS = [psM2[0:1, 4 * n:4 * n + 4, :].rearrange("p a b -> p (a b)")[:, 0:NQ // 2] for n in range(2)]

        s_const = sem("s_const")
        s_ioc = sem("s_ioc")
        s_prep = sem("s_prep")
        s_wT = sem("s_wT")
        b_be = sem("b_be")
        b_in = [sem(f"b_in{h}") for h in range(3)]
        b_add = sem("b_add")
        b_out = sem("b_out")
        s_bn = sem("s_bn")
        s_ready = sem("s_ready")
        s_ea = [sem(f"s_ea{b}") for b in range(2)]
        s_ix = [sem(f"s_ix{b}") for b in range(2)]
        s_xg = [sem(f"s_xg{b}") for b in range(2)]
        s_tr = [sem(f"s_tr{b}") for b in range(2)]
        s_eaT = sem("s_eaT")
        s_mm = sem("s_mm")
        s_pre = [sem(f"s_pre{b}") for b in range(2)]
        s_msg = sem("s_msg")
        s_rel = sem("s_rel")
        s_hot = sem("s_hot")
        s_seg = sem("s_seg")
        s_acc = sem("s_acc")
        s_chk = sem("s_chk")
        s_chkp = sem("s_chkp")
        s_flag = sem("s_flag")
        g_in = [sem(f"g_in{l}") for l in range(2)]
        g_xg = [sem(f"g_xg{l}") for l in range(2)]
        g_tr = sem("g_tr")
        g_eaT = sem("g_eaT")
        g_mm = sem("g_mm")
        g_pre = sem("g_pre")
        g_msg = sem("g_msg")
        g_z = [sem(f"g_z{l}") for l in range(2)]
        g_df = [sem(f"g_df{l}") for l in range(2)]
        g_hot = [sem(f"g_hot{l}") for l in range(2)]
        g_seg = [sem(f"g_seg{l}") for l in range(2)]
        g_acc = [sem(f"g_acc{l}") for l in range(2)]
        e_clr = sem("e_clr")
        e_row = sem("e_row")
        e_f = sem("e_f")
        e_tr = sem("e_tr")
        e_cp = sem("e_cp")
        e_nm = sem("e_nm")
        e_bl = sem("e_bl")
        e_cnt = sem("e_cnt")
        e_rot = sem("e_rot")
        e_bs = sem("e_bs")
        e_st = sem("e_st")
        c_key = sem("c_key")
        c_hot = sem("c_hot")
        c_mm = sem("c_mm")
        c_ev = sem("c_ev")
        c_st = [sem(f"c_st{b}") for b in range(2)]
        p_sp = sem("p_sp")
        p_ld = [sem(f"p_ld{k}") for k in range(NP_)]
        p_us = sem("p_us")
        p_ev = sem("p_ev")
        s_flag2 = sem("s_flag2")
        n_x = [[sem(f"n_x{k}{b}") for b in range(2)] for k in range(3)]
        n_xT = [sem(f"n_xT{k}") for k in range(3)]
        n_hT = [sem(f"n_hT{k}") for k in range(3)]
        n_h1 = sem("n_h1")
        n_a1 = sem("n_a1")
        n_h2 = [sem(f"n_h2{k}") for k in range(3)]
        n_a = sem("n_a")
        n_b = sem("n_b")
        n_sa = sem("n_sa")
        n_sb = sem("n_sb")
        n_xp = sem("n_xp")
        n_p0 = sem("n_p0")
        n_ch = [None] + [sem(f"n_ch{k}") for k in (1, 2)]
        n_sq = [None] + [sem(f"n_sq{k}") for k in (1, 2)]
        n_aT = [None] + [sem(f"n_aT{k}") for k in (1, 2)]
        n_out = [[sem(f"n_out{k}{b}") for b in range(2)] for k in range(3)]
        s_through = sem("s_through")
        s_acc0 = sem("s_acc0")
        s_clr = sem("s_clr")
        s_mask = sem("s_mask")
        g_mask = [sem(f"g_mask{l}") for l in range(2)]
        s_done = sem("s_done")

        psT_node = psT2[:, 0:TC, 0:NT]
        psN_node = psN[:, 0:TC, 0:NT]
        psM_node = psM2[0:NT, 0:TC, :]

        block = ctx.enter_context(nc.Block())

        def later(value):
            return not isinstance(value, int) or value > 0

        def edges(t, off):
            return t[bass.ds(off, GE)].rearrange("(p j) -> p j", j=J)

        def attrs(off):
            return ea[bass.ds(off, GE), :].rearrange("(p j) d -> p (j d)", j=J)

        def group_offset(i, b, last):
            return E - GE if last and b == 1 else i * (2 * GE) + b * GE

        def node_rows(t, c):
            return t[bass.ds(c * CN, CN), :].rearrange("(t p) d -> p t d", p=NT)

        SMALL = 3 + 2 + 6 + 3

        @block.sync
        def _(sp):
            sp.dma_start(be_bc[:, :], be.rearrange("(o d) -> o d", o=1).broadcast_to([P, D])).then_inc(b_be, 16)
            halves = [t[0:XR * P, :].rearrange("(p h r) d -> p h r d", p=P, h=2) for t in (x, xb_dram)]
            for h in range(2):
                sp.dma_start(xh[h], halves[0][:, h, :, :]).then_inc(b_in[h], 16)
            sp.dma_start(xr, x[XR * P:N, :]).then_inc(b_in[2], 16)
            sp.wait_ge(e_clr, 2)
            cut = KFULL * P * P
            for rows_i, t in ((drow_i, dst), (srow_i, src)):
                sp.dma_start(rows_i[:, 0:KFULL * P].rearrange("p (c e) -> p c e", c=KFULL),
                             t[0:cut].rearrange("(c p e) -> p c e", p=P, e=P)).then_inc(e_row, 16)
                sp.dma_start(rows_i[0:KT - KFULL * P, KFULL * P:KPAD],
                             t[cut:KT * P].rearrange("(p e) -> p e", e=P)).then_inc(e_row, 16)
                sp.dma_start(rows_i[KT - KFULL * P:KT - KFULL * P + 1, KFULL * P:KFULL * P + KREM],
                             t[KT * P:E].rearrange("(o e) -> o e", o=1)).then_inc(e_row, 16)
            for h in range(2):
                sp.wait_ge(b_add, h + 1)
                sp.dma_start(halves[1][:, h, :, :], xh[h]).then_inc(b_out, 16)
            sp.wait_ge(b_add, 3)
            sp.dma_start(xb_dram[XR * P:N, :], xr).then_inc(b_out, 16)
            sp.dma_start(bases[0:1, 1:G].unsqueeze(2),
                         dst[0:(G - 1) * GE].rearrange("(o g e) -> o g e", o=1, e=GE)[:, :, 0:1],
                         allow_slow_non_contiguous=True).then_inc(e_bs, 16)
            sp.dma_start(bases[0:1, G:G + 1], dst[E - GE:E - GE + 1].rearrange("(o e) -> o e", o=1)).then_inc(e_bs, 16)

            def load(i, b, last):
                off = group_offset(i, b, last)
                if later(16 * J * i):
                    sp.wait_ge(s_xg[b], 16 * J * i)
                sp.dma_start(srci[b][:, :], edges(src, off)).then_inc(s_ix[b], 16)
                if later(6 * i + 3 * b - 3):
                    sp.wait_ge(s_rel, 6 * i + (3 * b - 3))
                sp.dma_start(dsti[b][:, :], edges(dst, off)).then_inc(s_ea[b], 16)
                if later(H * i):
                    sp.wait_ge(s_tr[b], H * i)
                sp.dma_start(ea_sb[b][:, :, :].rearrange("p j d -> p (j d)"), attrs(off)).then_inc(s_ea[b], 16)

            for b in range(2):
                load(0, b, False)
            with sp.Fori(1, PAIRS - 1) as i:
                for b in range(2):
                    load(i, b, False)
            for b in range(2):
                load(PAIRS - 1, b, True)

            def general_loads(l, sp_off, g):
                if later(g * NW):
                    sp.wait_ge(g_acc[l], g * NW)
                sp.dma_start(srci[0][:, :], edges(src, sp_off)).then_inc(g_in[l], 16)
                sp.dma_start(dsti[0][:, :], edges(dst, sp_off)).then_inc(g_in[l], 16)
                if l == 0:
                    sp.dma_start(ea_sb[0][:, :, :].rearrange("p j d -> p (j d)"), attrs(sp_off)).then_inc(g_in[l], 16)

            def general_body(l):
                general_loads(l, 0, 0)
                with sp.Fori(1, G - 1) as g:
                    general_loads(l, g * GE, g)
                general_loads(l, E - GE, G - 1)

            sp.wait_ge(s_flag, 1)
            v = sp.value_load(flag[0:1, 0:1], min_val=0, max_val=1)
            with sp.If(v == 1):
                general_body(0)

            sp.wait_ge(s_done, 1)
            for b in range(2):
                sp.wait_ge(c_st[b], 16 * PAIRS)

            def count_load(c, h, k):
                if later(c * (2 * NP_) + (h * NP_ + k - NP_ + 1)):
                    sp.wait_ge(p_us, c * (2 * NP_) + (h * NP_ + k - NP_ + 1))
                sp.dma_start(piece[k][:, :, :, :],
                             counts[bass.ds(c * (2 * DG) + h * DG, DG), :, k * HP * GW:(k + 1) * HP * GW]
                             .rearrange("g p (t n) -> p g t n", t=HP)).then_inc(p_ld[k], 16)

            def node_load(i, b):
                sp.dma_start(xc[b][:, :, :], node_rows(x, i * 2 + b)).then_inc(n_x[0][b], 16)

            def node_store(c, b):
                sp.wait_ge(n_b, c * CO + CO)
                sp.dma_start(node_rows(x2_dram, c), oc[b][:, :, :]).then_inc(n_out[0][b], 16)

            for b in range(2):
                node_load(0, b)
            for k in range(NP_):
                count_load(0, 0, k)

            def step(i, b, first, last):
                c = i * 2 + b
                if not first:
                    node_store(c - 1, 1 - b)
                if not last:
                    sp.wait_ge(n_a, c * CA + CA)
                    node_load(i + 1, b)

            for b in range(2):
                step(0, b, b == 0, False)
            with sp.Fori(1, CPAIRS - 1) as i:
                for b in range(2):
                    step(i, b, False, False)
            for b in range(2):
                step(CPAIRS - 1, b, False, True)
            node_store(2 * CPAIRS - 1, 1)

            for h in range(2):
                for k in range(NP_):
                    if h == 1:
                        if k == NP_ - 1:
                            sp.wait_ge(p_us, EARLY + NP_)
                        count_load(0, h, k)
            with sp.Fori(1, DC) as c:
                for h in range(2):
                    for k in range(NP_):
                        count_load(c, h, k)
            sp.wait_ge(s_flag2, 1)
            v = sp.value_load(flag2[0:1, 0:1], min_val=0, max_val=1)
            with sp.If(v == 1):
                sp.wait_ge(p_ev, 2 * DC)
                general_body(1)

        @block.gpsimd
        def _(pool):
            pool.memset(ident[:, :], 0.0).then_inc(s_ioc, 1)
            pool.memset(keep[:, :], 1.0).then_inc(s_ioc, 1)
            pool.memset(ones_col[:, :], 1.0).then_inc(s_ioc, 1)
            pool.wait_ge(s_ioc, 3)
            pool.affine_select(out=ident[:, :], in_=ident[:, :], compare_op=ALU.not_equal, fill=1.0, base=0,
                               pattern=[[-1, P]], channel_multiplier=1).then_inc(s_ioc, 1)
            pool.affine_select(out=keep[:, :], in_=keep[:, :], compare_op=ALU.is_ge, fill=0.0, base=-DUP,
                               pattern=[[1, J]], channel_multiplier=J).then_inc(s_ioc, 1)
            pool.iota(iota16[:, :], [[1, NQ]], base=0, channel_multiplier=0,
                      allow_small_or_imprecise_dtypes=True).then_inc(s_ioc, 1)
            pool.iota(tab[:, :], [[1, CB]], base=1, channel_multiplier=0,
                      allow_small_or_imprecise_dtypes=True).then_inc(s_ioc, 1)
            pool.iota(tab0[:, :, :], [[1, P], [0, QT]], base=0, channel_multiplier=0,
                      allow_small_or_imprecise_dtypes=True).then_inc(s_ioc, 1)
            pool.iota(iota[:, :], [[1, NPAD]], base=0, channel_multiplier=0,
                      allow_small_or_imprecise_dtypes=True).then_inc(s_ioc, 1)
            pool.wait_ge(b_out, 48)

            def gather(table, idx, rows_, signal):
                pool.sem_inc(s_through, 1)
                for j in range(J):
                    pool.indirect_dma_start(rows_[:, j, :], None, table,
                                            bass.IndirectOffsetOnAxis(ap=idx[:, j:j + 1], axis=0)).then_inc(signal, 16)

            def group(i, b):
                pool.wait_ge(s_ix[b], 16 * i + 16)
                if later(H * i):
                    pool.wait_ge(s_pre[b], H * i)
                gather(xb_dram[:, :], srci[b], xg[b], s_xg[b])

            for b in range(2):
                group(0, b)
            pool.wait_ge(e_nm, 14)
            pool.memset(acc[:, :], 0.0).then_inc(s_clr, 1)
            with pool.Fori(1, PAIRS) as i:
                for b in range(2):
                    group(i, b)

            def general_body(l, table):
                def group(g):
                    pool.wait_ge(g_in[l], g * (48 - 16 * l) + (48 - 16 * l))
                    if later(g * NW):
                        pool.wait_ge(g_acc[l], g * NW)
                    gather(table, srci[0], xg[0], g_xg[l])

                group(0)
                with pool.Fori(1, G) as g:
                    group(g)

            pool.wait_ge(s_flag, 1)
            v = pool.value_load(flag[0:1, 0:1], min_val=0, max_val=1)
            with pool.If(v == 1):
                general_body(0, xb_dram[:, :])

            pool.wait_ge(s_done, 1)

            def shifted(i, b):
                pool.wait_ge(n_x[0][b], 16 * i + 16)
                if later(i * (2 * CA) + (b - 2) * CA + 9):
                    pool.wait_ge(n_a, i * (2 * CA) + ((b - 2) * CA + 9))
                pool.sem_inc(s_through, 1)
                pool.tensor_add(z[:, 6 + b, :, :], xc[b][:, :, :],
                                rows[0:NT, 2, :].unsqueeze(1).broadcast_to([NT, TC, D])).then_inc(n_xp, 1)

            def split(c, b):
                part = [parts[:, k, bass.ds(c * TC, TC), :] for k in range(3)]
                pool.wait_ge(n_p0, c + 1)
                pool.sem_inc(s_through, 1)
                pool.tensor_sub(rest[0], oc[b][:, :, :], part[0]).then_inc(p_sp, 1)
                pool.wait_ge(p_sp, c * 4 + 1)
                pool.tensor_copy(part[1], rest[0]).then_inc(p_sp, 1)
                pool.wait_ge(p_sp, c * 4 + 2)
                pool.sem_inc(s_through, 1)
                pool.tensor_sub(rest[1], rest[0], part[1]).then_inc(p_sp, 1)
                pool.wait_ge(p_sp, c * 4 + 3)
                pool.tensor_copy(part[2], rest[1]).then_inc(p_sp, 1)

            def step(i, b, first, last):
                if not last:
                    shifted(i + b, 1 - b)
                if not first:
                    split(i * 2 + (b - 1), 1 - b)

            shifted(0, 0)
            for b in range(2):
                step(0, b, b == 0, False)
            with pool.Fori(1, CPAIRS - 1) as i:
                for b in range(2):
                    step(i, b, False, False)
            for b in range(2):
                step(CPAIRS - 1, b, False, b == 1)
            split(2 * CPAIRS - 1, 1)
            for b in range(2):
                pool.wait_ge(n_out[0][b], 16 * CPAIRS)

            def nodes(k):
                def step(i):
                    for b in range(2):
                        if later(16 * i):
                            pool.wait_ge(n_out[k][b], 16 * i)
                        pool.sem_inc(s_through, 1)
                        pool.dma_start(xc[b][:, :, :], node_rows(x2_dram, i * 2 + b)).then_inc(n_x[k][b], 16)
                    for b in range(2):
                        c = i * 2 + b
                        pool.wait_ge(n_ch[k], c * CH + CH)
                        pool.sem_inc(s_through, 1)
                        pool.dma_start(node_rows(out, c), oc[b][:, :, :]).then_inc(n_out[k][b], 16)

                step(0)
                with pool.Fori(1, CPAIRS) as i:
                    step(i)
                for b in range(2):
                    pool.wait_ge(n_out[k][b], 16 * CPAIRS)

            nodes(1)
            pool.wait_ge(s_flag2, 1)
            v = pool.value_load(flag2[0:1, 0:1], min_val=0, max_val=1)
            with pool.If(v == 1):
                general_body(1, x2_dram[:, :])
                nodes(2)

        @block.scalar
        def _(act):
            for k, w in enumerate((We, W1, W2)):
                act.dma_start(wrow[:, k, :], w).then_inc(s_const, 16)
            act.dma_start(Wm_sb[:, :], Wm).then_inc(s_const, 16)
            act.dma_start(Ws_sb[:, :], Wself).then_inc(s_const, 16)
            for k, v in enumerate((b1, bn_g, bn_b, bn_rm, bn_rv)):
                act.dma_start(cols[:, k:k + 1], v.rearrange("(p o) -> p o", o=1)).then_inc(s_const, 16)
            act.dma_start(cols[:, 5:6], eps.rearrange("(a o) -> a o", o=1).broadcast_to([P, 1])).then_inc(s_const, 16)
            for k, v in enumerate((b2, ln_g, ln_b)):
                act.dma_start(rows[:, k, :], v.rearrange("(o d) -> o d", o=1).broadcast_to([P, D])).then_inc(s_const, 16)
            act.wait_ge(s_prep, 2)
            nc.scalar.activation(bn_t[:, 1:2], bn_t[:, 0:1], ACT.Sqrt).then_inc(s_bn, 1)
            for n_, (out_, ps_) in enumerate(((srow[:, 0:J * P], psT2[:, :, :]),
                                              (srow[:, J * P:KPAD], psC2[:, 0:KC - J, :]),
                                              (drow[:, 0:J * P], psM2[:, :, :]),
                                              (drow[:, J * P:KPAD], psT2[:, 0:KC - J, :]))):
                act.wait_ge(e_tr, n_ + 1)
                nc.scalar.copy(out_.rearrange("p (c e) -> p c e", e=P), ps_).then_inc(e_cp, 1)

            for a, done in ((0, 7), (2, 11), (1, 14)):
                act.wait_ge(e_nm, done)
                for sh in range(1, SH):
                    k = sh * SE
                    to = sh * PLANE + a * KPAD
                    act.dma_start(num[0:P - k, to:to + KPAD],
                                  num[k:P, a * KPAD:(a + 1) * KPAD]).then_inc(e_rot, 16)
                    act.dma_start(num[P - k:P, to:to + KPAD - 1],
                                  num[0:k, a * KPAD + 1:(a + 1) * KPAD]).then_inc(e_rot, 16)

            def attributes(i, b):
                for h in range(H):
                    act.wait_ge(s_tr[b], H * i + h + 1)
                    if later(4 * i + 2 * b):
                        act.wait_ge(s_mm, 4 * i + 2 * b)
                    nc.scalar.copy(eaT[h][:, :, :], psT[h][:, :, :]).then_inc(s_eaT, 1)

            def group(i, b, following):
                g = i * 2 + b
                if later(16 * i):
                    act.wait_ge(c_st[b], 16 * i)
                for q in range(QG):
                    act.wait_ge(c_mm, g * QG + (q + 1))
                    nc.scalar.copy(cbuf[b][:, :, q * QN:(q + 1) * QN],
                                   psC[q % 2].rearrange("p (t n) -> p t n", t=HN)).then_inc(c_ev, 1)
                    if q == 1 and following:
                        attributes(i + b, 1 - b)
                for h in range(H):
                    act.wait_ge(s_pre[b], H * i + h + 1)
                    if later(2 * i + b):
                        act.wait_ge(s_seg, 2 * i + b)
                    nc.scalar.activation(msg[h][:, :, :], pre[h][:, :, :], ACT.Relu).then_inc(s_msg, 1)
                act.wait_ge(c_ev, g * QG + QG)
                act.dma_start(counts[bass.ds(g, 1), :, :].rearrange("g p f -> (g p) f"),
                              cbuf[b][:, :, :].rearrange("p t n -> p (t n)")).then_inc(c_st[b], 16)

            attributes(0, 0)
            for b in range(2):
                group(0, b, True)
            with act.Fori(1, PAIRS - 1) as i:
                for b in range(2):
                    group(i, b, True)
            for b in range(2):
                group(PAIRS - 1, b, b == 0)

            act.wait_ge(s_flag, 1)
            v = act.value_load(flag[0:1, 0:1], min_val=0, max_val=1)
            with act.If(v == 1):
                def general_group(g):
                    for h in range(H):
                        act.wait_ge(g_tr, g * H + (h + 1))
                        if later(g * H):
                            act.wait_ge(g_mm, g * H)
                        nc.scalar.copy(eaT[h][:, :, :], psT[h][:, :, :]).then_inc(g_eaT, 1)
                    for h in range(H):
                        act.wait_ge(g_pre, g * H + (h + 1))
                        if later(g * NW):
                            act.wait_ge(g_seg[0], g * NW)
                        nc.scalar.activation(msg[h][:, :, :], pre[h][:, :, :], ACT.Relu).then_inc(g_msg, 1)

                general_group(0)
                with act.Fori(1, G) as g:
                    general_group(g)

            def hidden(c):
                act.wait_ge(n_h1, c + 1)
                if later(c):
                    act.wait_ge(n_h2[0], c)
                nc.scalar.activation(aT[:, :, :], psT_node, ACT.Relu, bias=bn_bias[:, :],
                                     scale=bn_scale[:, :]).then_inc(n_a1, 1)

            def step(c, b, first, last):
                if not first:
                    act.wait_ge(n_b, c * CO + (3 - CO))
                    nc.scalar.activation(z[:, 4, :, :], z[:, 3, :, :], ACT.Square).then_inc(n_sb, 1)
                act.wait_ge(n_a, c * CA + 4)
                nc.scalar.activation(z[:, 1, :, :], z[:, 0, :, :], ACT.Square).then_inc(n_sa, 1)
                if not first:
                    act.wait_ge(n_b, c * CO + (5 - CO))
                    nc.scalar.activation(st[:, 10, :], st[:, 9, :], ACT.Sqrt).then_inc(n_sb, 1)
                act.wait_ge(n_a, c * CA + 6)
                nc.scalar.activation(st[:, 4, :], st[:, 3, :], ACT.Sqrt).then_inc(n_sa, 1)
                if not last:
                    hidden(c + 1)
                if not first:
                    first_part(c - 1, 1 - b)

            def first_part(c, b):
                act.wait_ge(n_b, c * CO + CO)
                nc.scalar.copy(parts[:, 0, bass.ds(c * TC, TC), :], oc[b][:, :, :]).then_inc(n_p0, 1)

            hidden(0)
            for b in range(2):
                step(b, b, b == 0, False)
            with act.Fori(1, CPAIRS - 1) as i:
                for b in range(2):
                    step(i * 2 + b, b, False, False)
            for b in range(2):
                step(2 * CPAIRS - 2 + b, b, False, b == 1)
            act.wait_ge(n_b, 2 * CPAIRS * CO - 4)
            nc.scalar.activation(z[:, 4, :, :], z[:, 3, :, :], ACT.Square).then_inc(n_sb, 1)
            act.wait_ge(n_b, 2 * CPAIRS * CO - 2)
            nc.scalar.activation(st[:, 10, :], st[:, 9, :], ACT.Sqrt).then_inc(n_sb, 1)
            first_part(2 * CPAIRS - 1, 1)

            def evacuate(c, h):
                act.wait_ge(p_us, c * (2 * NP_) + NP_ * (h + 1))
                nc.scalar.copy(acc[:, bass.ds(c * (2 * DG * GW) + h * DG * GW, DG * GW)],
                               psA[h][:, 0:DG * GW]).then_inc(p_ev, 1)

            def rows_T(k, c):
                act.wait_ge(n_xT[k], c + 1)
                if later(c):
                    act.wait_ge(n_h2[k], c)
                nc.scalar.copy(aT[:, :, :], psN_node).then_inc(n_aT[k], 1)

            def norm(k, c):
                act.wait_ge(n_ch[k], c * CH + 4)
                nc.scalar.activation(z[:, 1, :, :], z[:, 0, :, :], ACT.Square).then_inc(n_sq[k], 1)
                act.wait_ge(n_ch[k], c * CH + 6)
                nc.scalar.activation(st[:, 4, :], st[:, 3, :], ACT.Sqrt).then_inc(n_sq[k], 1)

            def dense(c):
                evacuate(c, 0)
                rows_T(1, c - 1)
                evacuate(c, 1)
                norm(1, c - 1)

            act.wait_ge(p_us, EARLY + NP_)
            for h in range(2):
                evacuate(0, h)
            dense(1)
            with act.Fori(2, DC) as c:
                dense(c)
            rows_T(1, DC - 1)
            norm(1, DC - 1)

            act.wait_ge(s_flag2, 1)
            v = act.value_load(flag2[0:1, 0:1], min_val=0, max_val=1)
            with act.If(v == 1):
                rows_T(2, 0)
                norm(2, 0)
                with act.Fori(1, DC) as c:
                    rows_T(2, c)
                    norm(2, c)

        @block.vector
        def _(dve):
            nc.vector.memset(drow_i, -1).then_inc(e_clr, 1)
            nc.vector.memset(srow_i, -1).then_inc(e_clr, 1)
            nc.vector.memset(found[:, :], 0.0).then_inc(s_acc0, 1)
            nc.vector.memset(bases[0:1, 0:1], 0).then_inc(s_acc0, 1)
            nc.vector.memset(vmax[:, :], 0.0).then_inc(s_acc0, 1)
            nc.vector.memset(vmin[:, :], 0.0).then_inc(s_acc0, 1)
            dve.wait_ge(b_be, 16)
            for h in range(2):
                dve.wait_ge(b_in[h], 16)
                nc.vector.tensor_add(xh[h], xh[h], be_bc[:, :].unsqueeze(1).broadcast_to([P, XR // 2, D])).then_inc(b_add, 1)
            dve.wait_ge(b_in[2], 16)
            nc.vector.tensor_add(xr, xr, be_bc[0:N - XR * P, :]).then_inc(b_add, 1)
            dve.wait_ge(s_const, 16 * SMALL)
            n = [0]

            def prep(ins):
                n[0] += 1
                ins.then_inc(s_prep, 1)
                dve.wait_ge(s_prep, n[0])

            prep(nc.vector.tensor_scalar(one_eps[:, :], cols[:, 5:6], 1.0, None, ALU.add))
            prep(nc.vector.tensor_scalar(bn_t[:, 0:1], cols[:, 4:5], EPS, None, ALU.add))
            dve.wait_ge(s_bn, 1)
            prep(nc.vector.reciprocal(bn_t[:, 2:3], bn_t[:, 1:2]))
            prep(nc.vector.tensor_mul(bn_scale[:, :], bn_t[:, 2:3], cols[:, 1:2]))
            prep(nc.vector.tensor_sub(bn_t[:, 3:4], cols[:, 0:1], cols[:, 3:4]))
            prep(nc.vector.scalar_tensor_tensor(out=bn_bias[:, :], in0=bn_t[:, 3:4], scalar=bn_scale[:, :],
                                                in1=cols[:, 2:3], op0=ALU.mult, op1=ALU.add))
            dve.wait_ge(s_ioc, 5)
            prep(nc.vector.tensor_scalar(keep1[:, :], keep[:, :], -1.0, None, ALU.add))
            dve.wait_ge(s_wT, 1)
            for k, t in enumerate((WeT, W1T, W2T)):
                nc.vector.tensor_copy(t[:, :], psT[0][:, k, :]).then_inc(s_ready, 1)

            dve.wait_ge(e_row, 96)
            nc.vector.tensor_copy(srow_f, srow_i).then_inc(e_f, 1)
            nc.vector.tensor_copy(drow_f, drow_i).then_inc(e_f, 1)
            dve.wait_ge(e_f, 2)
            m = [0]

            def number(ins):
                m[0] += 1
                ins.then_inc(e_nm, 1)
                dve.wait_ge(e_nm, m[0])

            number(nc.vector.tensor_scalar(fb[:, :], drow_f.rearrange("p (u e) -> p u e", e=SE)[:, :, 0],
                                           1.0 / QN, 0.5 / QN - 0.5, ALU.mult, ALU.add))
            number(nc.vector.tensor_scalar(fb[:, :], fb[:, :], ROUND, None, ALU.add))
            number(nc.vector.tensor_scalar(fb[:, :], fb[:, :], -ROUND, None, ALU.add))
            dve.wait_ge(s_ioc, 6)
            for n_ in range(KC * SH):
                if n_ >= SLOTS:
                    dve.wait_ge(e_cnt, n_ - SLOTS + 1)
                nc.vector.tensor_scalar(below[n_ % SLOTS], iota16[:, :], fb[:, n_:n_ + 1], None,
                                        ALU.is_gt).then_inc(e_bl, 1)
            numv = num[:, 0:PLANE]
            dve.wait_ge(b_out, 48)
            dve.wait_ge(e_cp, 2)
            number(nc.vector.tensor_scalar(lo_f, srow, 1.0 / NT, 0.5 / NT - 0.5, ALU.mult, ALU.add))
            number(nc.vector.tensor_scalar(kk_f, lo_f, ROUND, None, ALU.add))
            number(nc.vector.tensor_scalar(kk_f, kk_f, -ROUND, None, ALU.add))
            number(nc.vector.scalar_tensor_tensor(out=numv[:, 0:KPAD], in0=kk_f, scalar=-float(NT), in1=srow,
                                                  op0=ALU.mult, op1=ALU.add))
            dve.wait_ge(e_cp, 4)
            number(nc.vector.tensor_scalar(srow, drow, 1.0 / QN, 0.5 / QN - 0.5, ALU.mult, ALU.add))
            number(nc.vector.tensor_scalar(srow, srow, ROUND, None, ALU.add))
            number(nc.vector.tensor_scalar(srow, srow, -ROUND, None, ALU.add))
            number(nc.vector.tensor_copy(numv[:, 2 * KPAD:3 * KPAD], srow))
            number(nc.vector.scalar_tensor_tensor(out=drow, in0=srow, scalar=-float(QN), in1=drow,
                                                  op0=ALU.mult, op1=ALU.add))
            number(nc.vector.scalar_tensor_tensor(out=kk_f, in0=kk_f, scalar=float(QN), in1=drow,
                                                  op0=ALU.mult, op1=ALU.add))
            number(nc.vector.tensor_scalar(numv[:, KPAD:2 * KPAD], kk_f, 1.0, None, ALU.add))
            dve.wait_ge(e_cnt, KC * SH)
            for n_ in range(2):
                nc.vector.tensor_scalar(starts_f[:, n_ * (NQ // 2):(n_ + 1) * (NQ // 2)], psS[n_],
                                        -float(UPAD + 1), 0.0, ALU.add, ALU.max).then_inc(e_st, 1)
            dve.wait_ge(e_st, 2)
            w_ = [2]

            def start(ins):
                w_[0] += 1
                ins.then_inc(e_st, 1)
                dve.wait_ge(e_st, w_[0])

            start(nc.vector.tensor_scalar(starts_f, starts_f, float(UMAX), None, ALU.min))
            start(nc.vector.tensor_scalar(starts_k, starts_f, 1.0 / SH, 0.5 / SH - 0.5, ALU.mult, ALU.add))
            start(nc.vector.tensor_scalar(starts_k, starts_k, ROUND, None, ALU.add))
            start(nc.vector.tensor_scalar(starts_k, starts_k, -ROUND, None, ALU.add))
            start(nc.vector.scalar_tensor_tensor(out=starts_s, in0=starts_k, scalar=-float(SH), in1=starts_f,
                                                 op0=ALU.mult, op1=ALU.add))
            start(nc.vector.scalar_tensor_tensor(out=starts[:, :], in0=starts_s, scalar=float(PLANE), in1=starts_k,
                                                 op0=ALU.mult, op1=ALU.add))
            dve.wait_ge(e_rot, 16 * 6 * (SH - 1))
            dve.wait_ge(e_bs, 32)
            dve.wait_ge(s_acc0, 4)
            dve.wait_ge(s_ioc, 9)

            def keys(g, b, first):
                for q in range(QG):
                    ins = nc.vector.scalar_tensor_tensor(
                        out=key[b][:, q * QT:(q + 1) * QT], in0=num[:, bass.ds(first[q] + 2 * KPAD, QT)],
                        scalar=iota[:, bass.ds(g * QG + q, 1)], in1=num[:, bass.ds(first[q] + KPAD, QT)],
                        op0=ALU.is_equal, op1=ALU.mult)
                ins.then_inc(c_key, 1)

            def block(g, b, q, first):
                if later(g * QG + (q + 1 - QG)):
                    dve.wait_ge(c_mm, g * QG + (q + 1 - QG))
                nc.vector.tensor_tensor(Lh[q], tab0[:, :, :],
                                        num[:, bass.ds(first[q], QT)].unsqueeze(1).broadcast_to([P, P, QT]),
                                        ALU.is_equal)
                for t in range(QT):
                    ins = nc.vector.tensor_scalar(Rh[q][:, t, :], tab[:, :], key[b][:, q * QT + t:q * QT + t + 1],
                                                  None, ALU.is_equal)
                ins.then_inc(c_hot, 1)

            hot_in1 = iota[:, 0:W].unsqueeze(1).broadcast_to([P, J, W])

            def loads(i):
                _, base = nc.values_load_multi_w_load_instructions(
                    bases[0:1, bass.ds(i * 2, 3)], engines=[mybir.EngineType.DVE], min_val=0, max_val=N - 1)
                _, first = nc.values_load_multi_w_load_instructions(
                    starts[0:1, bass.ds(i * (2 * QG), 2 * QG)], engines=[mybir.EngineType.DVE], min_val=0,
                    max_val=(SH - 1) * PLANE + KT + 1 - QT)
                return base, first

            def masked(where, signal):
                nc.vector.tensor_mul(relm[:, 0, :], where, keep[:, :]).then_inc(signal, 1)
                dve.wait_ge(signal, 1)
                nc.vector.tensor_add(relm[:, 1, :], relm[:, 0, :], keep1[:, :]).then_inc(signal, 1)
                dve.wait_ge(signal, 2)
                return relm[:, 1, :]

            def add(g, base):
                dve.wait_ge(s_seg, g + 1)
                if later(g):
                    dve.wait_ge(s_acc, g)
                else:
                    dve.wait_ge(s_clr, 1)
                nc.vector.tensor_add(acc[:, bass.ds(base, W)], acc[:, bass.ds(base, W)],
                                     psA[0][:, 0:W]).then_inc(s_acc, 1)

            def adds(i, b):
                g = i * 2 + b
                dve.wait_ge(s_xg[b], 16 * J * i + 16 * J)
                if later(2 * g):
                    dve.wait_ge(s_msg, 2 * g)
                for h in range(H):
                    dve.wait_ge(s_mm, g * 2 + (h + 1))
                    nc.vector.tensor_add(pre[h][:, :, :], psM[h][:, :, :],
                                         xg[b][:, h * JH:(h + 1) * JH, :]).then_inc(s_pre[b], 1)

            def front(i, b, last, base, first):
                g = i * 2 + b
                dve.wait_ge(s_ea[b], 32 * i + 32)
                if later(g):
                    dve.wait_ge(s_hot, g)
                nc.vector.tensor_scalar(rel[:, :], dsti[b][:, :], iota[:, bass.ds(base[b + 1], 1)], None,
                                        ALU.subtract).then_inc(s_rel, 1)
                keys(g, b, first)
                dve.wait_ge(s_rel, g * 3 + 1)
                nc.vector.tensor_tensor(vmax[:, :], vmax[:, :], rel[:, :], ALU.max).then_inc(s_rel, 1)
                nc.vector.tensor_tensor(vmin[:, :], vmin[:, :], rel[:, :], ALU.min).then_inc(s_rel, 1)
                dve.wait_ge(c_key, g * 2 + 1)
                nc.vector.scalar_tensor_tensor(out=found[:, :], in0=key[b][:, :], scalar=1.0, in1=found[:, :],
                                               op0=ALU.min, op1=ALU.add).then_inc(c_key, 1)
                block(g, b, 0, first)
                dve.wait_ge(s_rel, g * 3 + 3)
                block(g, b, 1, first)
                block(g, b, 2, first)
                if b == 0:
                    adds(i, 0)
                block(g, b, 3, first)
                if later(g):
                    add(g - 1, base[b])
                where = masked(rel[:, :], s_mask) if last and b == 1 else rel[:, :]
                nc.vector.tensor_tensor(hot[:, :, :], where.unsqueeze(2).broadcast_to([P, J, W]), hot_in1,
                                        ALU.is_equal).then_inc(s_hot, 1)

            def pair(i, last):
                if later(i):
                    adds(i - 1, 1)
                base, first = loads(i)
                front(i, 0, last, base, first[0:QG])
                front(i, 1, last, base, first[QG:2 * QG])
                return base[2]

            pair(0, False)
            with dve.Fori(1, PAIRS - 1) as i:
                pair(i, False)
            base = pair(PAIRS - 1, True)
            adds(PAIRS - 1, 1)
            add(G - 1, base)

            k = [0]

            def chk(ins):
                k[0] += 1
                ins.then_inc(s_chk, 1)
                dve.wait_ge(s_chk, k[0])

            chk(nc.vector.tensor_reduce(viol[:, 0:1], vmax[:, :], axis=AX, op=ALU.max))
            chk(nc.vector.tensor_reduce(viol[:, 1:2], vmin[:, :], axis=AX, op=ALU.min))
            chk(nc.vector.tensor_scalar(viol[:, 2:3], viol[:, 0:1], float(-(W - 1)), None, ALU.add))
            chk(nc.vector.tensor_scalar(viol[:, 3:4], viol[:, 1:2], -1.0, None, ALU.mult))
            chk(nc.vector.tensor_max(viol[:, 0:1], viol[:, 2:3], viol[:, 3:4]))
            chk(nc.vector.tensor_reduce(fcol[:, 0:1], found[:, :], axis=AX, op=ALU.add))
            dve.wait_ge(s_chkp, 1)
            chk(nc.vector.tensor_reduce(flag_f[:, 1:2], psA[1][0:1, P:2 * P], axis=AX, op=ALU.add))
            nc.vector.tensor_scalar(flag2[:, :], flag_f[:, 1:2], float(E), None, ALU.not_equal).then_inc(s_flag2, 1)
            chk(nc.vector.tensor_reduce(flag_f[:, 0:1], psA[1][0:1, 0:P], axis=AX, op=ALU.max))
            nc.vector.tensor_scalar(flag[:, :], flag_f[:, 0:1], 0.0, None, ALU.is_gt).then_inc(s_flag, 1)

            def general_group(l, g, last):
                dve.wait_ge(g_in[l], g * (48 - 16 * l) + (48 - 16 * l))
                if later(g * NW):
                    dve.wait_ge(g_acc[l], g * NW)
                nc.vector.tensor_copy(dstf[:, 0, :], dsti[0][:, :]).then_inc(g_df[l], 1)
                dve.wait_ge(g_df[l], g + 1)
                where = masked(dstf[:, 0, :], g_mask[l]) if last else dstf[:, 0, :]
                if l == 0:
                    dve.wait_ge(g_xg[l], g * (16 * J) + 16 * J)
                    if later(g * H):
                        dve.wait_ge(g_msg, g * H)
                    for h in range(H):
                        dve.wait_ge(g_mm, g * H + (h + 1))
                        nc.vector.tensor_add(pre[h][:, :, :], psM[h][:, :, :],
                                             xg[0][:, h * JH:(h + 1) * JH, :]).then_inc(g_pre, 1)
                dve.sem_inc(s_through, 1)
                with dve.Fori(0, NW) as w:
                    nc.vector.tensor_tensor(whot[:, :, :], where.unsqueeze(2).broadcast_to([P, J, WW]),
                                            iota[:, bass.ds(w * WW, WW)].unsqueeze(1).broadcast_to([P, J, WW]),
                                            ALU.is_equal).then_inc(g_hot[l], 1)
                    dve.wait_ge(g_seg[l], g * NW + w + 1)
                    nc.vector.tensor_add(acc[:, bass.ds(w * WW, WW)], acc[:, bass.ds(w * WW, WW)],
                                         psA[0][:, :]).then_inc(g_acc[l], 1)
                    dve.wait_ge(g_acc[l], g * NW + w + 1)

            def general_body(l):
                nc.vector.memset(acc[:, :], 0.0).then_inc(g_z[l], 1)
                dve.wait_ge(g_z[l], 1)
                general_group(l, 0, False)
                with dve.Fori(1, G - 1) as g:
                    general_group(l, g, False)
                general_group(l, G - 1, True)
                dve.wait_ge(g_acc[l], G * NW)

            dve.wait_ge(s_acc, G)
            dve.wait_ge(s_flag, 1)
            v = dve.value_load(flag[0:1, 0:1], min_val=0, max_val=1)
            with dve.If(v == 1):
                general_body(0)
            for b in range(2):
                dve.wait_ge(c_st[b], 16 * PAIRS)
            nc.vector.memset(st[:, 12, :], 0.0).then_inc(s_done, 1)

            def per_row(col):
                return st[:, col, :].unsqueeze(2).broadcast_to([NT, TC, D])

            def chunk_sums(c):
                return acc[:, bass.ds(c * CN, CN)].rearrange("d (t n) -> d t n", t=TC)

            def input_T(c):
                dve.wait_ge(n_xT[0], c + 1)
                if later(c):
                    dve.wait_ge(n_h1, c)
                nc.vector.scalar_tensor_tensor(out=hT[:, :, :], in0=psN_node, scalar=one_eps[:, :],
                                               in1=chunk_sums(c), op0=ALU.mult, op1=ALU.add).then_inc(n_hT[0], 1)

            def step(c, b, first, last, tail):
                A, B = not tail, not first
                if A:
                    dve.wait_ge(n_h2[0], c + 1)
                    if later(c * CA):
                        dve.wait_ge(n_a, c * CA)
                    nc.vector.tensor_add(z[:, 2, :, :], psM_node,
                                         rows[0:NT, 0, :].unsqueeze(1).broadcast_to([NT, TC, D])).then_inc(n_a, 1)
                if B:
                    dve.wait_ge(n_a, c * CA)
                    nc.vector.tensor_reduce(st[:, 6, :], z[:, 5, :, :], axis=AX, op=ALU.add).then_inc(n_b, 1)
                if A:
                    dve.wait_ge(n_a, c * CA + 1)
                    nc.vector.tensor_reduce(st[:, 0, :], z[:, 2, :, :], axis=AX, op=ALU.add).then_inc(n_a, 1)
                if B:
                    dve.wait_ge(n_b, c * CO + (1 - CO))
                    nc.vector.tensor_scalar(st[:, 7, :], st[:, 6, :], 1.0 / D, None, ALU.mult).then_inc(n_b, 1)
                if A:
                    dve.wait_ge(n_a, c * CA + 2)
                    nc.vector.tensor_scalar(st[:, 1, :], st[:, 0, :], 1.0 / D, None, ALU.mult).then_inc(n_a, 1)
                if B:
                    dve.wait_ge(n_b, c * CO + (2 - CO))
                    nc.vector.tensor_sub(z[:, 3, :, :], z[:, 5, :, :], per_row(7)).then_inc(n_b, 1)
                if A:
                    dve.wait_ge(n_a, c * CA + 3)
                    nc.vector.tensor_sub(z[:, 0, :, :], z[:, 2, :, :], per_row(1)).then_inc(n_a, 1)
                if A and not last:
                    input_T(c + 1)
                if B:
                    dve.wait_ge(n_sb, c * 2 - 1)
                    nc.vector.tensor_reduce(st[:, 8, :], z[:, 4, :, :], axis=AX, op=ALU.add).then_inc(n_b, 1)
                if A:
                    dve.wait_ge(n_sa, c * 2 + 1)
                    nc.vector.tensor_reduce(st[:, 2, :], z[:, 1, :, :], axis=AX, op=ALU.add).then_inc(n_a, 1)
                if B:
                    dve.wait_ge(n_b, c * CO + (4 - CO))
                    nc.vector.tensor_scalar(st[:, 9, :], st[:, 8, :], 1.0 / D, EPS, ALU.mult,
                                            ALU.add).then_inc(n_b, 1)
                if A:
                    dve.wait_ge(n_a, c * CA + 5)
                    nc.vector.tensor_scalar(st[:, 3, :], st[:, 2, :], 1.0 / D, EPS, ALU.mult,
                                            ALU.add).then_inc(n_a, 1)
                if B:
                    dve.wait_ge(n_sb, c * 2)
                    nc.vector.reciprocal(st[:, 11, :], st[:, 10, :]).then_inc(n_b, 1)
                if A:
                    dve.wait_ge(n_sa, c * 2 + 2)
                    nc.vector.reciprocal(st[:, 5, :], st[:, 4, :]).then_inc(n_a, 1)
                if B:
                    dve.wait_ge(n_b, c * CO + (6 - CO))
                    if later(c - 2):
                        dve.wait_ge(n_out[0][1 - b], c * 8 + (b * 8 - 16))
                        dve.wait_ge(p_sp, c * 4 - 11)
                    nc.vector.tensor_mul(oc[1 - b][:, :, :], z[:, 3, :, :], per_row(11)).then_inc(n_b, 1)
                if A:
                    dve.wait_ge(n_a, c * CA + 7)
                    for t in range(TC):
                        ins = nc.vector.scalar_tensor_tensor(out=z[:, 2, t, :], in0=z[:, 0, t, :],
                                                             scalar=st[:, 5, t:t + 1], in1=rows[0:NT, 1, :],
                                                             op0=ALU.mult, op1=ALU.mult)
                    ins.then_inc(n_a, 1)
                    dve.wait_ge(n_a, c * CA + 8)
                    dve.wait_ge(n_xp, c + 1)
                    nc.vector.tensor_add(z[:, 0, :, :], z[:, 2, :, :], z[:, 6 + b, :, :]).then_inc(n_a, 1)
                    dve.wait_ge(n_a, c * CA + 9)
                    if B:
                        dve.wait_ge(n_b, c * CO)
                    nc.vector.scalar_tensor_tensor(out=z[:, 5, :, :], in0=z[:, 0, :, :], scalar=0.0,
                                                   in1=xc[b][:, :, :], op0=ALU.max, op1=ALU.add).then_inc(n_a, 1)

            input_T(0)
            for c in range(4):
                step(c, c % 2, c == 0, False, False)
            with dve.Fori(2, CPAIRS - 1) as i:
                for b in range(2):
                    step(i * 2 + b, b, False, False, False)
            for b in range(2):
                step(2 * CPAIRS - 2 + b, b, False, b == 1, False)
            step(2 * CPAIRS, 0, False, True, True)

            def node2(k, i, b):
                c = i * 2 + b
                m = [0]

                def link(ins):
                    m[0] += 1
                    ins.then_inc(n_ch[k], 1)
                    dve.wait_ge(n_ch[k], c * CH + m[0])

                if k == 1:
                    dve.wait_ge(p_ev, c * 2 + 2)
                if later(c):
                    dve.wait_ge(n_h2[k], c)
                nc.vector.tensor_copy(hT[:, :, :], chunk_sums(c)).then_inc(n_hT[k], 1)
                dve.wait_ge(n_h2[k], c + 1)
                link(nc.vector.tensor_add(z[:, 2, :, :], psM_node, xc[b][:, :, :]))
                link(nc.vector.tensor_reduce(st[:, 0, :], z[:, 2, :, :], axis=AX, op=ALU.add))
                link(nc.vector.tensor_scalar(st[:, 1, :], st[:, 0, :], 1.0 / D, None, ALU.mult))
                link(nc.vector.tensor_sub(z[:, 0, :, :], z[:, 2, :, :], per_row(1)))
                dve.wait_ge(n_sq[k], c * 2 + 1)
                link(nc.vector.tensor_reduce(st[:, 2, :], z[:, 1, :, :], axis=AX, op=ALU.add))
                link(nc.vector.tensor_scalar(st[:, 3, :], st[:, 2, :], 1.0 / D, EPS, ALU.mult, ALU.add))
                dve.wait_ge(n_sq[k], c * 2 + 2)
                link(nc.vector.reciprocal(st[:, 5, :], st[:, 4, :]))
                if later(16 * i):
                    dve.wait_ge(n_out[k][b], 16 * i)
                link(nc.vector.tensor_mul(oc[b][:, :, :], z[:, 0, :, :], per_row(5)))

            def nodes(k):
                for b in range(2):
                    node2(k, 0, b)
                with dve.Fori(1, CPAIRS) as i:
                    for b in range(2):
                        node2(k, i, b)

            for b in range(2):
                dve.wait_ge(n_out[0][b], 16 * CPAIRS)
            dve.wait_ge(p_sp, 4 * DC)
            nodes(1)
            dve.wait_ge(s_flag2, 1)
            v = dve.value_load(flag2[0:1, 0:1], min_val=0, max_val=1)
            with dve.If(v == 1):
                general_body(1)
                for b in range(2):
                    dve.wait_ge(n_out[1][b], 16 * CPAIRS)
                nodes(2)

        @block.tensor
        def _(pe):
            pe.wait_ge(s_const, 16 * SMALL)
            pe.wait_ge(s_ioc, 4)
            for k in range(3):
                last_ = nc.tensor.transpose(psT[0][:, k, :], wrow[:, k, :], ident[:, :])
            last_.then_inc(s_wT, 1)
            pe.wait_ge(s_ready, 3)
            pe.wait_ge(e_f, 2)
            for n_, (in_, c0, out_) in enumerate(((srow_f, 0, psT2), (srow_f, J, psC2),
                                                  (drow_f, 0, psM2), (drow_f, J, psT2))):
                if n_ == 3:
                    pe.wait_ge(e_cp, 1)
                for c in range(c0, min(c0 + J, KC)):
                    ins = nc.tensor.transpose(out_[:, c - c0, :], in_[:, c * P:(c + 1) * P], ident[:, :])
                ins.then_inc(e_tr, 1)
            pe.wait_ge(e_cp, 3)
            for c in range(KC * SH):
                pe.wait_ge(e_bl, c + 1)
                for n_ in range(2):
                    ins = nc.tensor.matmul(psS[n_], ones_col[:, :], below[c % SLOTS][:, n_ * (NQ // 2):(n_ + 1) * (NQ // 2)],
                                           start=c == 0, stop=c == KC * SH - 1)
                ins.then_inc(e_cnt, 1)
            pe.wait_ge(e_cp, 4)
            pe.wait_ge(e_st, 2)

            def block(g, q):
                pe.wait_ge(c_hot, g * QG + (q + 1))
                if later(g * QG + (q - 1)):
                    pe.wait_ge(c_ev, g * QG + (q - 1))
                for t in range(QT):
                    ins = nc.tensor.matmul(psC[q % 2], Lh[q][:, :, t], Rh[q][:, t, :], start=t == 0,
                                           stop=t == QT - 1)
                ins.then_inc(c_mm, 1)

            def transpose_group(b, signal):
                for h in range(H):
                    for j in range(JH):
                        ins = nc.tensor.transpose(psT[h][:, j, :], ea_sb[b][:, h * JH + j, :], ident[:, :])
                    ins.then_inc(signal, 1)

            def project(h, signal):
                for j in range(JH):
                    ins = nc.tensor.matmul(psM[h][:, j, :], eaT[h][:, j, :], WeT[:, :], start=True, stop=True)
                ins.then_inc(signal, 1)

            def attributes(i, b):
                g = i * 2 + b
                pe.wait_ge(s_ea[b], 32 * i + 32)
                if later(2 * g):
                    pe.wait_ge(s_eaT, 2 * g)
                transpose_group(b, s_tr[b])

            def products(i, b):
                g = i * 2 + b
                if later(H * (i + b)):
                    pe.wait_ge(s_pre[1 - b], H * (i + b))
                for h in range(H):
                    pe.wait_ge(s_eaT, g * 2 + (h + 1))
                    project(h, s_mm)

            def group(i, b, following):
                g = i * 2 + b
                for q in range(QG):
                    block(g, q)
                    if q == 1 and following:
                        attributes(i + b, 1 - b)
                if following:
                    products(i + b, 1 - b)
                pe.wait_ge(s_hot, g + 1)
                if later(g):
                    pe.wait_ge(s_acc, g)
                for h in range(H):
                    pe.wait_ge(s_msg, g * 2 + (h + 1))
                    for j in range(JH):
                        ins = nc.tensor.matmul(psA[0][:, 0:W], msg[h][:, j, :], hot[:, h * JH + j, :],
                                               start=h + j == 0, stop=h * JH + j == J - 1)
                ins.then_inc(s_seg, 1)

            attributes(0, 0)
            products(0, 0)
            for b in range(2):
                group(0, b, True)
            with pe.Fori(1, PAIRS - 1) as i:
                for b in range(2):
                    group(i, b, True)
            for b in range(2):
                group(PAIRS - 1, b, b == 0)

            pe.wait_ge(s_chk, 6)
            nc.tensor.matmul(psA[1][0:1, P:2 * P], fcol[:, 0:1], ident[:, :], start=True, stop=True)
            nc.tensor.matmul(psA[1][0:1, 0:P], viol[:, 0:1], ident[:, :], start=True, stop=True).then_inc(s_chkp, 1)

            def general_body(l):
                def group(g):
                    if l == 0:
                        pe.wait_ge(g_in[l], g * 48 + 48)
                        if later(g * H):
                            pe.wait_ge(g_eaT, g * H)
                        transpose_group(0, g_tr)
                        if later(g * H):
                            pe.wait_ge(g_pre, g * H)
                        for h in range(H):
                            pe.wait_ge(g_eaT, g * H + (h + 1))
                            project(h, g_mm)
                        pe.wait_ge(g_msg, g * H + H)
                    else:
                        pe.wait_ge(g_xg[l], g * (16 * J) + 16 * J)
                    pe.sem_inc(s_through, 1)
                    with pe.Fori(0, NW) as w:
                        pe.wait_ge(g_hot[l], g * NW + w + 1)
                        for j in range(J):
                            rows_ = msg[j // JH][:, j % JH, :] if l == 0 else xg[0][:, j, :]
                            ins = nc.tensor.matmul(psA[0][:, :], rows_, whot[:, j, :], start=j == 0,
                                                   stop=j == J - 1)
                        ins.then_inc(g_seg[l], 1)

                group(0)
                with pe.Fori(1, G) as g:
                    group(g)

            pe.wait_ge(s_flag, 1)
            v = pe.value_load(flag[0:1, 0:1], min_val=0, max_val=1)
            with pe.If(v == 1):
                general_body(0)

            def rows_T(k, i, b, reader):
                c = i * 2 + b
                pe.wait_ge(n_x[k][b], 16 * i + 16)
                if later(c):
                    pe.wait_ge(reader, c)
                for t in range(TC):
                    ins = nc.tensor.transpose(psN[:, t, 0:NT], xc[b][:, t, :], ident[0:NT, 0:NT])
                ins.then_inc(n_xT[k], 1)

            def step(i, b, last):
                c = i * 2 + b
                pe.wait_ge(n_hT[0], c + 1)
                if later(c):
                    pe.wait_ge(n_a1, c)
                for t in range(TC):
                    ins = nc.tensor.matmul(psT2[:, t, 0:NT], W1T[:, :], hT[:, t, :], start=True, stop=True)
                ins.then_inc(n_h1, 1)
                pe.wait_ge(n_a1, c + 1)
                if later(c * CA):
                    pe.wait_ge(n_a, c * CA + (1 - CA))
                for t in range(TC):
                    ins = nc.tensor.matmul(psM2[0:NT, t, :], aT[:, t, :], W2T[:, :], start=True, stop=True)
                ins.then_inc(n_h2[0], 1)
                if not last:
                    rows_T(0, i + b, 1 - b, n_hT[0])

            rows_T(0, 0, 0, n_hT[0])
            for b in range(2):
                step(0, b, False)
            with pe.Fori(1, CPAIRS - 1) as i:
                for b in range(2):
                    step(i, b, False)
            for b in range(2):
                step(CPAIRS - 1, b, b == 1)

            def dense(c, h, some=range(NP_)):
                if later(c * 2 + (h - 1)) and later(c):
                    pe.wait_ge(p_ev, c * 2 + (h - 1))
                for k in some:
                    pe.wait_ge(p_ld[k], c * 32 + 16 * (h + 1))
                    for t in range(HP):
                        for part in range(3):
                            ins = nc.tensor.matmul(
                                psA[h][:, 0:DG * GW].rearrange("p (g n) -> p g n", g=DG),
                                parts[:, part, k * HP + t, :], piece[k][0:NT, :, t, :],
                                start=k + t + part == 0, stop=k * HP + t == HN - 1 and part == 2)
                    ins.then_inc(p_us, 1)

            def products(k, c):
                pe.wait_ge(n_hT[k], c + 1)
                pe.wait_ge(n_aT[k], c + 1)
                if later(c * CH):
                    pe.wait_ge(n_ch[k], c * CH + (1 - CH))
                for t in range(TC):
                    nc.tensor.matmul(psM2[0:NT, t, :], hT[:, t, :], Wm_sb[:, :], start=True, stop=False)
                    ins = nc.tensor.matmul(psM2[0:NT, t, :], aT[:, t, :], Ws_sb[:, :], start=False, stop=True)
                ins.then_inc(n_h2[k], 1)

            def beside(i, b):
                dense(i * 2 + b, 0)
                rows_T(1, i + (b - 1), 1 - b, n_aT[1])
                dense(i * 2 + b, 1)
                products(1, i * 2 + (b - 1))

            for k in range(NP_ - 1):
                pe.wait_ge(p_sp, 4 * (HP // TC) * (k + 1))
                dense(0, 0, [k])
            dense(0, 1, range(EARLY))
            pe.wait_ge(p_sp, 4 * DC)
            dense(0, 0, [NP_ - 1])
            dense(0, 1, range(EARLY, NP_))
            beside(0, 1)
            with pe.Fori(1, CPAIRS) as i:
                for b in range(2):
                    beside(i, b)
            rows_T(1, CPAIRS - 1, 1, n_aT[1])
            products(1, DC - 1)

            pe.wait_ge(s_flag2, 1)
            v = pe.value_load(flag2[0:1, 0:1], min_val=0, max_val=1)
            with pe.If(v == 1):
                general_body(1)
                for b in range(2):
                    rows_T(2, 0, b, n_aT[2])
                    products(2, b)
                with pe.Fori(1, CPAIRS) as i:
                    for b in range(2):
                        rows_T(2, i, b, n_aT[2])
                        products(2, i * 2 + b)


_INS = ["x", "src", "dst", "edge_attr_128", "L0_gnn_eps", "L0_gnn_We", "L0_gnn_be", "L0_gnn_W1", "L0_gnn_b1",
        "L0_gnn_bn_g", "L0_gnn_bn_b", "L0_gnn_bn_rm", "L0_gnn_bn_rv", "L0_gnn_W2", "L0_gnn_b2", "L0_gnn_ln_g",
        "L0_gnn_ln_b", "L1_gnn_W", "L1_gnn_W_self"]


def kernel(**inputs):
    import concourse.bacc as bacc
    from concourse.bass_utils import run_bass_kernel_spmd

    nc = bacc.Bacc("TRN2", target_bir_lowering=False, num_devices=1)
    arrays, args = {}, []
    for name in _INS:
        a = np.ascontiguousarray(inputs[name])
        if a.ndim == 0:
            a = a.reshape(1)
        arrays[f"in_{name}"] = a
        args.append(nc.dram_tensor(f"in_{name}", a.shape, mybir.dt.from_np(a.dtype), kind="ExternalInput").ap())
    n = inputs["x"].shape[0]
    out = nc.dram_tensor("out_rows", (n, D), F32, kind="ExternalOutput").ap()
    program(nc, *args, out)
    r = run_bass_kernel_spmd(nc, [arrays], core_ids=[0])
    return r.results[0]["out_rows"]
```
